# Optimizing a Trainium2 kernel written in Bass

```python
import numpy as np
import jax
import jax.numpy as jnp

def _softmax(x, axis=-1):
    return jax.nn.softmax(x, axis=axis)

def _gelu(x):
    return jax.nn.gelu(x, approximate=True)

def _silu(x):
    return jax.nn.silu(x)

def _sigmoid(x):
    return jax.nn.sigmoid(x)

def _layernorm(x, axis=-1, eps=1e-05):
    m = jnp.mean(x, axis=axis, keepdims=True)
    v = jnp.var(x, axis=axis, keepdims=True)
    return (x - m) / jnp.sqrt(v + eps)

def _scatter_add(tgt, idx, src, axis=0):
    return tgt.at[idx].add(src)

def _segment_sum(src, seg, n):
    return jax.ops.segment_sum(src, seg, n)
kernel_name = 'mk_xattn_seq_d4_seqx_r8_5ddc14'

def setup_inputs(seed: int=0):
    np.random.seed(seed)
    _w = jnp.asarray

    def _rec_inputs():
        import jax
        import jax.numpy as jnp
        _rk = jax.random.key(seed)
        x = -0.0005207 + 1.001 * jax.random.normal(jax.random.fold_in(_rk, 1), (4, 256, 256), jnp.float32)
        _lenS = 256 - jax.random.randint(jax.random.fold_in(_rk, 7), (4,), 0, max(1, 256 // 4) + 1, jnp.int32)
        _lenS2 = 256 - jax.random.randint(jax.random.fold_in(_rk, 8), (4,), 0, max(1, 256 // 4) + 1, jnp.int32)
        _ctx_2048P = jax.random.normal(jax.random.fold_in(_rk, 11), (4, 16, 256), jnp.float32)
        _ctx_2048c = jax.random.dirichlet(jax.random.fold_in(_rk, 511), 0.3 * jnp.ones((16,), jnp.float32), (4, 256))
        _ctx_2048t = jnp.einsum('bsk,bkd->bsd', _ctx_2048c, _ctx_2048P)
        _ctx_2048t = _ctx_2048t * jax.lax.rsqrt(jnp.mean(jnp.square(_ctx_2048t)) + 1e-12) * 0.953939
        ctx_2048 = 2.81802e-05 + 1.00001 * (_ctx_2048t + 0.3 * jax.random.normal(jax.random.fold_in(_rk, 611), (4, 256, 256), jnp.float32))
        _validS = jnp.arange(256)[None, :] < _lenS[:, None]
        _validS2 = jnp.arange(256)[None, :] < _lenS2[:, None]
        _causal = jnp.tril(jnp.ones((256, 256), dtype=bool))
        mask_BxS2_bf1 = jnp.ones((4, 256), dtype=bool)
        mask_BxS2_ik0 = jnp.where(jnp.broadcast_to(_validS2[:, :], (4, 256)), 0, 1).astype(jnp.int32)
        mask_Bx1xSxS2_ff0 = jnp.where(jnp.ones((4, 1, 256, 256), dtype=bool), 0.0, -1000000000.0).astype(jnp.float32)
        return (x, ctx_2048, mask_BxS2_bf1, mask_BxS2_ik0, mask_Bx1xSxS2_ff0)
    x, ctx_2048, mask_BxS2_bf1, mask_BxS2_ik0, mask_Bx1xSxS2_ff0 = _rec_inputs()

    def _L0_xattn_setup():
        import jax, jax.numpy as jnp
        import numpy as np
        B, Q, S1, S2 = (4, 32, 256, 256)
        D, H, K, F = (256, 16, 128, 1024)
        LN_EPS = 1e-05

        def _layer_norm(x, scale, offset):
            mu = jnp.mean(x, axis=-1, keepdims=True)
            var = jnp.var(x, axis=-1, keepdims=True)
            return (x - mu) * jax.lax.rsqrt(var + LN_EPS) * scale + offset

        def _cross_attention(q_in, kv_in, wq, bq, wk, bk, wv, bv, wo, bo, bias_k, bias_v):
            b, q_len, _ = q_in.shape
            t = kv_in.shape[1]
            qh = (q_in @ wq + bq).reshape(b, q_len, H, K)
            kh = (kv_in @ wk + bk).reshape(b, t, H, K)
            vh = (kv_in @ wv + bv).reshape(b, t, H, K)
            kh = jnp.concatenate([kh, jnp.broadcast_to(bias_k, (b, 1, H, K))], axis=1)
            vh = jnp.concatenate([vh, jnp.broadcast_to(bias_v, (b, 1, H, K))], axis=1)
            scale = jnp.sqrt(jnp.asarray(K, q_in.dtype))
            logits = jnp.einsum('bqhk,bthk->bhqt', qh, kh) / scale
            weights = jax.nn.softmax(logits, axis=-1)
            ctx = jnp.einsum('bhqt,bthk->bqhk', weights, vh).reshape(b, q_len, H * K)
            return ctx @ wo + bo

        def _forward(x, xf_1, xf_2, ln1_scale, ln1_offset, wq1, bq1, wk1, bk1, wv1, bv1, wo1, bo1, bias_k1, bias_v1, ln2_scale, ln2_offset, wq2, bq2, wk2, bk2, wv2, bv2, wo2, bo2, bias_k2, bias_v2, ln_mlp_scale, ln_mlp_offset, w_fc1, b_fc1, w_fc2, b_fc2):
            res = x
            h = _layer_norm(x, ln1_scale, ln1_offset)
            x = res + _cross_attention(h, xf_1, wq1, bq1, wk1, bk1, wv1, bv1, wo1, bo1, bias_k1, bias_v1)
            res = x
            h = _layer_norm(x, ln2_scale, ln2_offset)
            x = res + _cross_attention(h, xf_2, wq2, bq2, wk2, bk2, wv2, bv2, wo2, bo2, bias_k2, bias_v2)
            h = _layer_norm(x, ln_mlp_scale, ln_mlp_offset)
            h = jax.nn.gelu(h @ w_fc1 + b_fc1, approximate=False) @ w_fc2 + b_fc2
            return x + h
        key = jax.random.key(seed)
        ks = iter(jax.random.split(key, 64))

        def rn(shape, s=0.02):
            return jax.random.normal(next(ks), shape, jnp.float32) * s
        inp = {'x': rn((B, Q, D), 1.0), 'xf_1': rn((B, S1, D), 1.0), 'xf_2': rn((B, S2, D), 1.0)}
        for i in (1, 2):
            inp[f'ln{i}_scale'] = jnp.ones((D,), jnp.float32)
            inp[f'ln{i}_offset'] = jnp.zeros((D,), jnp.float32)
            inp[f'wq{i}'] = rn((D, H * K))
            inp[f'bq{i}'] = jnp.zeros((H * K,), jnp.float32)
            inp[f'wk{i}'] = rn((D, H * K))
            inp[f'bk{i}'] = jnp.zeros((H * K,), jnp.float32)
            inp[f'wv{i}'] = rn((D, H * K))
            inp[f'bv{i}'] = jnp.zeros((H * K,), jnp.float32)
            inp[f'wo{i}'] = rn((H * K, D))
            inp[f'bo{i}'] = jnp.zeros((D,), jnp.float32)
            inp[f'bias_k{i}'] = rn((1, 1, H, K))
            inp[f'bias_v{i}'] = rn((1, 1, H, K))
        inp['ln_mlp_scale'] = jnp.ones((D,), jnp.float32)
        inp['ln_mlp_offset'] = jnp.zeros((D,), jnp.float32)
        inp['w_fc1'] = rn((D, F))
        inp['b_fc1'] = jnp.zeros((F,), jnp.float32)
        inp['w_fc2'] = rn((F, D))
        inp['b_fc2'] = jnp.zeros((D,), jnp.float32)
        return inp
    _L0_xattn_all = _L0_xattn_setup()
    _L0_xattn_in = {k: v for k, v in _L0_xattn_all.items() if k in ('ln1_scale', 'ln1_offset', 'wq1', 'bq1', 'wk1', 'bk1', 'wv1', 'bv1', 'wo1', 'bo1', 'bias_k1', 'bias_v1', 'ln2_scale', 'ln2_offset', 'wq2', 'bq2', 'wk2', 'bk2', 'wv2', 'bv2', 'wo2', 'bo2', 'bias_k2', 'bias_v2', 'ln_mlp_scale', 'ln_mlp_offset', 'w_fc1', 'b_fc1', 'w_fc2', 'b_fc2')}
    del _L0_xattn_all

    def _L1_xattn_setup():
        import jax, jax.numpy as jnp
        import numpy as np
        D = 256
        H = 16
        HD = D // H
        INNER = 4 * D
        EPS = 1e-05

        def layer_norm(x, w, b):
            mu = jnp.mean(x, axis=-1, keepdims=True)
            var = jnp.mean(jnp.square(x - mu), axis=-1, keepdims=True)
            return (x - mu) * jax.lax.rsqrt(var + EPS) * w + b
        key = jax.random.key(seed)
        ks = jax.random.split(key, 12)
        B, LQ, LK = (4, 128, 256)
        std = 0.02
        inp = {'hidden_states': jax.random.normal(ks[0], (B, LQ, D), jnp.float32), 'encoder_hidden_states': jax.random.normal(ks[1], (B, LK, D), jnp.float32), 'encoder_attention_mask': jnp.ones((B, LK), dtype=bool), 'ln1_w': jnp.ones((D,), jnp.float32), 'ln1_b': jnp.zeros((D,), jnp.float32), 'q_w': jax.random.normal(ks[2], (D, D), jnp.float32) * std, 'q_b': jnp.zeros((D,), jnp.float32), 'k_w': jax.random.normal(ks[3], (D, D), jnp.float32) * std, 'k_b': jnp.zeros((D,), jnp.float32), 'v_w': jax.random.normal(ks[4], (D, D), jnp.float32) * std, 'v_b': jnp.zeros((D,), jnp.float32), 'cproj_w': jax.random.normal(ks[5], (D, D), jnp.float32) * std, 'cproj_b': jnp.zeros((D,), jnp.float32), 'ln2_w': jnp.ones((D,), jnp.float32), 'ln2_b': jnp.zeros((D,), jnp.float32), 'fc_w': jax.random.normal(ks[6], (D, INNER), jnp.float32) * std, 'fc_b': jnp.zeros((INNER,), jnp.float32), 'proj_w': jax.random.normal(ks[7], (INNER, D), jnp.float32) * std, 'proj_b': jnp.zeros((D,), jnp.float32)}
        return inp
    _L1_xattn_all = _L1_xattn_setup()
    _L1_xattn_in = {k: v for k, v in _L1_xattn_all.items() if k in ('ln1_w', 'ln1_b', 'q_w', 'q_b', 'k_w', 'k_b', 'v_w', 'v_b', 'cproj_w', 'cproj_b', 'ln2_w', 'ln2_b', 'fc_w', 'fc_b', 'proj_w', 'proj_b')}
    del _L1_xattn_all

    def _L2_xattn_setup():
        import jax, jax.numpy as jnp
        import numpy as np
        B, P, K, H, NH = (4, 256, 32, 256, 16)
        DH = H // NH
        EPS = 1e-06

        def rmsnorm(x, w):
            var = jnp.mean(jnp.square(x), axis=-1, keepdims=True)
            return x * jax.lax.rsqrt(var + EPS) * w
        key = jax.random.key(seed)
        ks = jax.random.split(key, 12)
        s = 0.02
        return {'x': jax.random.normal(ks[0], (B, P, H), jnp.float32), 'latents': jax.random.normal(ks[1], (B, K, H), jnp.float32), 'attention_mask': jax.random.randint(ks[2], (B, P), 0, 2, jnp.int32), 'q_w': s * jax.random.normal(ks[3], (H, H), jnp.float32), 'q_b': jnp.zeros((H,), jnp.float32), 'kv_w': s * jax.random.normal(ks[4], (H, 2 * H), jnp.float32), 'kv_b': jnp.zeros((2 * H,), jnp.float32), 'out_w': s * jax.random.normal(ks[5], (H, H), jnp.float32), 'out_b': jnp.zeros((H,), jnp.float32), 'postnorm_w': jnp.ones((H,), jnp.float32), 'mlp_w1': s * jax.random.normal(ks[6], (H, 4 * H), jnp.float32), 'mlp_b1': jnp.zeros((4 * H,), jnp.float32), 'mlp_w2': s * jax.random.normal(ks[7], (4 * H, H), jnp.float32), 'mlp_b2': jnp.zeros((H,), jnp.float32)}
    _L2_xattn_all = _L2_xattn_setup()
    _L2_xattn_in = {k: v for k, v in _L2_xattn_all.items() if k in ('q_w', 'q_b', 'kv_w', 'kv_b', 'out_w', 'out_b', 'postnorm_w', 'mlp_w1', 'mlp_b1', 'mlp_w2', 'mlp_b2')}
    del _L2_xattn_all

    def _L3_xattn_setup():
        import jax, jax.numpy as jnp
        import numpy as np
        H = 256
        NH = 32
        KVH = 8
        HD = H // NH
        GROUPS = NH // KVH
        EPS = 1e-06
        B, L, S = (4, 128, 128)

        def _gqa_forward(hidden_state, encoder_hidden_state, encoder_attention_mask, Wq, bq, Wk, bk, Wv, bv, Wo, bo, gamma, beta):
            b, l, _ = hidden_state.shape
            s = encoder_hidden_state.shape[1]
            q = hidden_state @ Wq + bq
            k = encoder_hidden_state @ Wk + bk
            v = encoder_hidden_state @ Wv + bv
            q = q.reshape(b, l, KVH, GROUPS, HD).transpose(0, 2, 3, 1, 4)
            k = k.reshape(b, s, KVH, HD).transpose(0, 2, 1, 3)
            v = v.reshape(b, s, KVH, HD).transpose(0, 2, 1, 3)
            scale = 1.0 / jnp.sqrt(jnp.asarray(HD, q.dtype))
            scores = jnp.einsum('bkgld,bksd->bkgls', q, k) * scale
            scores = scores + encoder_attention_mask[:, :, None, :, :]
            attn = jax.nn.softmax(scores, axis=-1)
            out = jnp.einsum('bkgls,bksd->bkgld', attn, v)
            out = out.transpose(0, 3, 1, 2, 4).reshape(b, l, H)
            out = out @ Wo + bo
            x = out + hidden_state
            mu = jnp.mean(x, axis=-1, keepdims=True)
            var = jnp.var(x, axis=-1, keepdims=True)
            return (x - mu) * jax.lax.rsqrt(var + EPS) * gamma + beta
        key = jax.random.key(seed)
        ks = jax.random.split(key, 12)
        sd = 0.02
        return {'hidden_state': jax.random.normal(ks[0], (B, L, H), jnp.float32), 'encoder_hidden_state': jax.random.normal(ks[1], (B, S, H), jnp.float32), 'encoder_attention_mask': jnp.zeros((B, 1, L, S), jnp.float32), 'Wq': jax.random.normal(ks[2], (H, H), jnp.float32) * sd, 'bq': jnp.zeros((H,), jnp.float32), 'Wk': jax.random.normal(ks[3], (H, KVH * HD), jnp.float32) * sd, 'bk': jnp.zeros((KVH * HD,), jnp.float32), 'Wv': jax.random.normal(ks[4], (H, KVH * HD), jnp.float32) * sd, 'bv': jnp.zeros((KVH * HD,), jnp.float32), 'Wo': jax.random.normal(ks[5], (H, H), jnp.float32) * sd, 'bo': jnp.zeros((H,), jnp.float32), 'gamma': jnp.ones((H,), jnp.float32), 'beta': jnp.zeros((H,), jnp.float32)}
    _L3_xattn_all = _L3_xattn_setup()
    _L3_xattn_in = {k: v for k, v in _L3_xattn_all.items() if k in ('Wq', 'bq', 'Wk', 'bk', 'Wv', 'bv', 'Wo', 'bo', 'gamma', 'beta')}
    del _L3_xattn_all
    return {'x': x, 'ctx_2048': ctx_2048, 'mask_BxS2_bf1': mask_BxS2_bf1, 'mask_BxS2_ik0': mask_BxS2_ik0, 'mask_Bx1xSxS2_ff0': mask_Bx1xSxS2_ff0, 'L0_xattn_ln1_scale': _L0_xattn_in['ln1_scale'], 'L0_xattn_ln1_offset': _L0_xattn_in['ln1_offset'], 'L0_xattn_wq1': _L0_xattn_in['wq1'], 'L0_xattn_bq1': _L0_xattn_in['bq1'], 'L0_xattn_wk1': _L0_xattn_in['wk1'], 'L0_xattn_bk1': _L0_xattn_in['bk1'], 'L0_xattn_wv1': _L0_xattn_in['wv1'], 'L0_xattn_bv1': _L0_xattn_in['bv1'], 'L0_xattn_wo1': _L0_xattn_in['wo1'], 'L0_xattn_bo1': _L0_xattn_in['bo1'], 'L0_xattn_bias_k1': _L0_xattn_in['bias_k1'], 'L0_xattn_bias_v1': _L0_xattn_in['bias_v1'], 'L0_xattn_ln2_scale': _L0_xattn_in['ln2_scale'], 'L0_xattn_ln2_offset': _L0_xattn_in['ln2_offset'], 'L0_xattn_wq2': _L0_xattn_in['wq2'], 'L0_xattn_bq2': _L0_xattn_in['bq2'], 'L0_xattn_wk2': _L0_xattn_in['wk2'], 'L0_xattn_bk2': _L0_xattn_in['bk2'], 'L0_xattn_wv2': _L0_xattn_in['wv2'], 'L0_xattn_bv2': _L0_xattn_in['bv2'], 'L0_xattn_wo2': _L0_xattn_in['wo2'], 'L0_xattn_bo2': _L0_xattn_in['bo2'], 'L0_xattn_bias_k2': _L0_xattn_in['bias_k2'], 'L0_xattn_bias_v2': _L0_xattn_in['bias_v2'], 'L0_xattn_ln_mlp_scale': _L0_xattn_in['ln_mlp_scale'], 'L0_xattn_ln_mlp_offset': _L0_xattn_in['ln_mlp_offset'], 'L0_xattn_w_fc1': _L0_xattn_in['w_fc1'], 'L0_xattn_b_fc1': _L0_xattn_in['b_fc1'], 'L0_xattn_w_fc2': _L0_xattn_in['w_fc2'], 'L0_xattn_b_fc2': _L0_xattn_in['b_fc2'], 'L1_xattn_ln1_w': _L1_xattn_in['ln1_w'], 'L1_xattn_ln1_b': _L1_xattn_in['ln1_b'], 'L1_xattn_q_w': _L1_xattn_in['q_w'], 'L1_xattn_q_b': _L1_xattn_in['q_b'], 'L1_xattn_k_w': _L1_xattn_in['k_w'], 'L1_xattn_k_b': _L1_xattn_in['k_b'], 'L1_xattn_v_w': _L1_xattn_in['v_w'], 'L1_xattn_v_b': _L1_xattn_in['v_b'], 'L1_xattn_cproj_w': _L1_xattn_in['cproj_w'], 'L1_xattn_cproj_b': _L1_xattn_in['cproj_b'], 'L1_xattn_ln2_w': _L1_xattn_in['ln2_w'], 'L1_xattn_ln2_b': _L1_xattn_in['ln2_b'], 'L1_xattn_fc_w': _L1_xattn_in['fc_w'], 'L1_xattn_fc_b': _L1_xattn_in['fc_b'], 'L1_xattn_proj_w': _L1_xattn_in['proj_w'], 'L1_xattn_proj_b': _L1_xattn_in['proj_b'], 'L2_xattn_q_w': _L2_xattn_in['q_w'], 'L2_xattn_q_b': _L2_xattn_in['q_b'], 'L2_xattn_kv_w': _L2_xattn_in['kv_w'], 'L2_xattn_kv_b': _L2_xattn_in['kv_b'], 'L2_xattn_out_w': _L2_xattn_in['out_w'], 'L2_xattn_out_b': _L2_xattn_in['out_b'], 'L2_xattn_postnorm_w': _L2_xattn_in['postnorm_w'], 'L2_xattn_mlp_w1': _L2_xattn_in['mlp_w1'], 'L2_xattn_mlp_b1': _L2_xattn_in['mlp_b1'], 'L2_xattn_mlp_w2': _L2_xattn_in['mlp_w2'], 'L2_xattn_mlp_b2': _L2_xattn_in['mlp_b2'], 'L3_xattn_Wq': _L3_xattn_in['Wq'], 'L3_xattn_bq': _L3_xattn_in['bq'], 'L3_xattn_Wk': _L3_xattn_in['Wk'], 'L3_xattn_bk': _L3_xattn_in['bk'], 'L3_xattn_Wv': _L3_xattn_in['Wv'], 'L3_xattn_bv': _L3_xattn_in['bv'], 'L3_xattn_Wo': _L3_xattn_in['Wo'], 'L3_xattn_bo': _L3_xattn_in['bo'], 'L3_xattn_gamma': _L3_xattn_in['gamma'], 'L3_xattn_beta': _L3_xattn_in['beta']}

def reference(x, ctx_2048, mask_BxS2_bf1, mask_BxS2_ik0, mask_Bx1xSxS2_ff0, L0_xattn_ln1_scale, L0_xattn_ln1_offset, L0_xattn_wq1, L0_xattn_bq1, L0_xattn_wk1, L0_xattn_bk1, L0_xattn_wv1, L0_xattn_bv1, L0_xattn_wo1, L0_xattn_bo1, L0_xattn_bias_k1, L0_xattn_bias_v1, L0_xattn_ln2_scale, L0_xattn_ln2_offset, L0_xattn_wq2, L0_xattn_bq2, L0_xattn_wk2, L0_xattn_bk2, L0_xattn_wv2, L0_xattn_bv2, L0_xattn_wo2, L0_xattn_bo2, L0_xattn_bias_k2, L0_xattn_bias_v2, L0_xattn_ln_mlp_scale, L0_xattn_ln_mlp_offset, L0_xattn_w_fc1, L0_xattn_b_fc1, L0_xattn_w_fc2, L0_xattn_b_fc2, L1_xattn_ln1_w, L1_xattn_ln1_b, L1_xattn_q_w, L1_xattn_q_b, L1_xattn_k_w, L1_xattn_k_b, L1_xattn_v_w, L1_xattn_v_b, L1_xattn_cproj_w, L1_xattn_cproj_b, L1_xattn_ln2_w, L1_xattn_ln2_b, L1_xattn_fc_w, L1_xattn_fc_b, L1_xattn_proj_w, L1_xattn_proj_b, L2_xattn_q_w, L2_xattn_q_b, L2_xattn_kv_w, L2_xattn_kv_b, L2_xattn_out_w, L2_xattn_out_b, L2_xattn_postnorm_w, L2_xattn_mlp_w1, L2_xattn_mlp_b1, L2_xattn_mlp_w2, L2_xattn_mlp_b2, L3_xattn_Wq, L3_xattn_bq, L3_xattn_Wk, L3_xattn_bk, L3_xattn_Wv, L3_xattn_bv, L3_xattn_Wo, L3_xattn_bo, L3_xattn_gamma, L3_xattn_beta):
    import jax
    import jax.numpy as jnp

    def _L0_xattn_ref(x, xf_1, xf_2, ln1_scale, ln1_offset, wq1, bq1, wk1, bk1, wv1, bv1, wo1, bo1, bias_k1, bias_v1, ln2_scale, ln2_offset, wq2, bq2, wk2, bk2, wv2, bv2, wo2, bo2, bias_k2, bias_v2, ln_mlp_scale, ln_mlp_offset, w_fc1, b_fc1, w_fc2, b_fc2):
        import jax, jax.numpy as jnp
        import numpy as np
        B, Q, S1, S2 = (4, 32, 256, 256)
        D, H, K, F = (256, 16, 128, 1024)
        LN_EPS = 1e-05

        def _layer_norm(x, scale, offset):
            mu = jnp.mean(x, axis=-1, keepdims=True)
            var = jnp.var(x, axis=-1, keepdims=True)
            return (x - mu) * jax.lax.rsqrt(var + LN_EPS) * scale + offset

        def _cross_attention(q_in, kv_in, wq, bq, wk, bk, wv, bv, wo, bo, bias_k, bias_v):
            b, q_len, _ = q_in.shape
            t = kv_in.shape[1]
            qh = (q_in @ wq + bq).reshape(b, q_len, H, K)
            kh = (kv_in @ wk + bk).reshape(b, t, H, K)
            vh = (kv_in @ wv + bv).reshape(b, t, H, K)
            kh = jnp.concatenate([kh, jnp.broadcast_to(bias_k, (b, 1, H, K))], axis=1)
            vh = jnp.concatenate([vh, jnp.broadcast_to(bias_v, (b, 1, H, K))], axis=1)
            scale = jnp.sqrt(jnp.asarray(K, q_in.dtype))
            logits = jnp.einsum('bqhk,bthk->bhqt', qh, kh) / scale
            weights = jax.nn.softmax(logits, axis=-1)
            ctx = jnp.einsum('bhqt,bthk->bqhk', weights, vh).reshape(b, q_len, H * K)
            return ctx @ wo + bo

        def _forward(x, xf_1, xf_2, ln1_scale, ln1_offset, wq1, bq1, wk1, bk1, wv1, bv1, wo1, bo1, bias_k1, bias_v1, ln2_scale, ln2_offset, wq2, bq2, wk2, bk2, wv2, bv2, wo2, bo2, bias_k2, bias_v2, ln_mlp_scale, ln_mlp_offset, w_fc1, b_fc1, w_fc2, b_fc2):
            res = x
            h = _layer_norm(x, ln1_scale, ln1_offset)
            x = res + _cross_attention(h, xf_1, wq1, bq1, wk1, bk1, wv1, bv1, wo1, bo1, bias_k1, bias_v1)
            res = x
            h = _layer_norm(x, ln2_scale, ln2_offset)
            x = res + _cross_attention(h, xf_2, wq2, bq2, wk2, bk2, wv2, bv2, wo2, bo2, bias_k2, bias_v2)
            h = _layer_norm(x, ln_mlp_scale, ln_mlp_offset)
            h = jax.nn.gelu(h @ w_fc1 + b_fc1, approximate=False) @ w_fc2 + b_fc2
            return x + h
        return _forward(x, xf_1, xf_2, ln1_scale, ln1_offset, wq1, bq1, wk1, bk1, wv1, bv1, wo1, bo1, bias_k1, bias_v1, ln2_scale, ln2_offset, wq2, bq2, wk2, bk2, wv2, bv2, wo2, bo2, bias_k2, bias_v2, ln_mlp_scale, ln_mlp_offset, w_fc1, b_fc1, w_fc2, b_fc2)

    def _L1_xattn_ref(hidden_states, encoder_hidden_states, encoder_attention_mask, ln1_w, ln1_b, q_w, q_b, k_w, k_b, v_w, v_b, cproj_w, cproj_b, ln2_w, ln2_b, fc_w, fc_b, proj_w, proj_b):
        import jax, jax.numpy as jnp
        import numpy as np
        D = 256
        H = 16
        HD = D // H
        INNER = 4 * D
        EPS = 1e-05

        def layer_norm(x, w, b):
            mu = jnp.mean(x, axis=-1, keepdims=True)
            var = jnp.mean(jnp.square(x - mu), axis=-1, keepdims=True)
            return (x - mu) * jax.lax.rsqrt(var + EPS) * w + b
        B, LQ, _ = hidden_states.shape
        LK = encoder_hidden_states.shape[1]
        residual = hidden_states
        x = layer_norm(hidden_states, ln1_w, ln1_b)
        q = (x @ q_w + q_b).reshape(B, LQ, H, HD).transpose(0, 2, 1, 3)
        k = (encoder_hidden_states @ k_w + k_b).reshape(B, LK, H, HD).transpose(0, 2, 1, 3)
        v = (encoder_hidden_states @ v_w + v_b).reshape(B, LK, H, HD).transpose(0, 2, 1, 3)
        scale = 1.0 / np.sqrt(HD).astype(np.float32)
        scores = jnp.einsum('bhqd,bhkd->bhqk', q, k) * scale
        mask = encoder_attention_mask[:, None, None, :]
        mask_value = jnp.finfo(scores.dtype).min
        scores = jnp.where(mask, scores, mask_value)
        attn = jax.nn.softmax(scores, axis=-1)
        out = jnp.einsum('bhqk,bhkd->bhqd', attn, v)
        out = out.transpose(0, 2, 1, 3).reshape(B, LQ, D)
        out = out @ cproj_w + cproj_b
        hidden = out + residual
        residual = hidden
        y = layer_norm(hidden, ln2_w, ln2_b)
        y = jax.nn.gelu(y @ fc_w + fc_b, approximate=True)
        y = y @ proj_w + proj_b
        return residual + y

    def _L2_xattn_ref(x, latents, attention_mask, q_w, q_b, kv_w, kv_b, out_w, out_b, postnorm_w, mlp_w1, mlp_b1, mlp_w2, mlp_b2):
        import jax, jax.numpy as jnp
        import numpy as np
        B, P, K, H, NH = (4, 256, 32, 256, 16)
        DH = H // NH
        EPS = 1e-06

        def rmsnorm(x, w):
            var = jnp.mean(jnp.square(x), axis=-1, keepdims=True)
            return x * jax.lax.rsqrt(var + EPS) * w
        b, p, _ = x.shape
        k_len = latents.shape[1]
        residual = latents
        h = jnp.concatenate([x, latents], axis=1)
        q = (latents @ q_w + q_b).reshape(b, k_len, NH, DH)
        kv = (h @ kv_w + kv_b).reshape(b, p + k_len, NH, DH, 2)
        kmat, v = (kv[..., 0], kv[..., 1])
        attn = jnp.einsum('bkhd,bnhd->bhkn', q, kmat) / DH
        full_mask = jnp.concatenate([attention_mask.astype(bool), jnp.ones((b, k_len), bool)], axis=-1)
        attn = jnp.where(full_mask[:, None, None, :], attn, -jnp.inf)
        attn = jax.nn.softmax(attn.astype(jnp.float32), axis=-1).astype(q.dtype)
        attn_out = jnp.einsum('bhkn,bnhd->bkhd', attn, v).reshape(b, k_len, H)
        attn_out = attn_out @ out_w + out_b + residual
        out = rmsnorm(attn_out, postnorm_w)
        out = jax.nn.gelu(out @ mlp_w1 + mlp_b1) @ mlp_w2 + mlp_b2
        return out + residual

    def _L3_xattn_ref(hidden_state, encoder_hidden_state, encoder_attention_mask, Wq, bq, Wk, bk, Wv, bv, Wo, bo, gamma, beta):
        import jax, jax.numpy as jnp
        import numpy as np
        H = 256
        NH = 32
        KVH = 8
        HD = H // NH
        GROUPS = NH // KVH
        EPS = 1e-06
        B, L, S = (4, 128, 128)

        def _gqa_forward(hidden_state, encoder_hidden_state, encoder_attention_mask, Wq, bq, Wk, bk, Wv, bv, Wo, bo, gamma, beta):
            b, l, _ = hidden_state.shape
            s = encoder_hidden_state.shape[1]
            q = hidden_state @ Wq + bq
            k = encoder_hidden_state @ Wk + bk
            v = encoder_hidden_state @ Wv + bv
            q = q.reshape(b, l, KVH, GROUPS, HD).transpose(0, 2, 3, 1, 4)
            k = k.reshape(b, s, KVH, HD).transpose(0, 2, 1, 3)
            v = v.reshape(b, s, KVH, HD).transpose(0, 2, 1, 3)
            scale = 1.0 / jnp.sqrt(jnp.asarray(HD, q.dtype))
            scores = jnp.einsum('bkgld,bksd->bkgls', q, k) * scale
            scores = scores + encoder_attention_mask[:, :, None, :, :]
            attn = jax.nn.softmax(scores, axis=-1)
            out = jnp.einsum('bkgls,bksd->bkgld', attn, v)
            out = out.transpose(0, 3, 1, 2, 4).reshape(b, l, H)
            out = out @ Wo + bo
            x = out + hidden_state
            mu = jnp.mean(x, axis=-1, keepdims=True)
            var = jnp.var(x, axis=-1, keepdims=True)
            return (x - mu) * jax.lax.rsqrt(var + EPS) * gamma + beta
        return _gqa_forward(hidden_state, encoder_hidden_state, encoder_attention_mask, Wq, bq, Wk, bk, Wv, bv, Wo, bo, gamma, beta)
    x = _L0_xattn_ref(x, ctx_2048, ctx_2048, L0_xattn_ln1_scale, L0_xattn_ln1_offset, L0_xattn_wq1, L0_xattn_bq1, L0_xattn_wk1, L0_xattn_bk1, L0_xattn_wv1, L0_xattn_bv1, L0_xattn_wo1, L0_xattn_bo1, L0_xattn_bias_k1, L0_xattn_bias_v1, L0_xattn_ln2_scale, L0_xattn_ln2_offset, L0_xattn_wq2, L0_xattn_bq2, L0_xattn_wk2, L0_xattn_bk2, L0_xattn_wv2, L0_xattn_bv2, L0_xattn_wo2, L0_xattn_bo2, L0_xattn_bias_k2, L0_xattn_bias_v2, L0_xattn_ln_mlp_scale, L0_xattn_ln_mlp_offset, L0_xattn_w_fc1, L0_xattn_b_fc1, L0_xattn_w_fc2, L0_xattn_b_fc2)
    x = _L1_xattn_ref(x, ctx_2048, mask_BxS2_bf1, L1_xattn_ln1_w, L1_xattn_ln1_b, L1_xattn_q_w, L1_xattn_q_b, L1_xattn_k_w, L1_xattn_k_b, L1_xattn_v_w, L1_xattn_v_b, L1_xattn_cproj_w, L1_xattn_cproj_b, L1_xattn_ln2_w, L1_xattn_ln2_b, L1_xattn_fc_w, L1_xattn_fc_b, L1_xattn_proj_w, L1_xattn_proj_b)
    x = _L2_xattn_ref(ctx_2048, x, mask_BxS2_ik0, L2_xattn_q_w, L2_xattn_q_b, L2_xattn_kv_w, L2_xattn_kv_b, L2_xattn_out_w, L2_xattn_out_b, L2_xattn_postnorm_w, L2_xattn_mlp_w1, L2_xattn_mlp_b1, L2_xattn_mlp_w2, L2_xattn_mlp_b2)
    x = _L3_xattn_ref(x, ctx_2048, mask_Bx1xSxS2_ff0, L3_xattn_Wq, L3_xattn_bq, L3_xattn_Wk, L3_xattn_bk, L3_xattn_Wv, L3_xattn_bv, L3_xattn_Wo, L3_xattn_bo, L3_xattn_gamma, L3_xattn_beta)
    return x

_drawn_inputs = setup_inputs


def setup_inputs(seed=0):
    import zlib

    import numpy as np

    out = dict(_drawn_inputs(seed))
    spreads = {'L0_xattn_ln1_scale': (1.0, 0.6),
     'L0_xattn_ln1_offset': (0.0, 0.8),
     'L0_xattn_bq1': (0.0, 0.8),
     'L0_xattn_bk1': (0.0, 2.0),
     'L0_xattn_bv1': (0.0, 0.1),
     'L0_xattn_bo1': (0.0, 0.1),
     'L0_xattn_ln2_scale': (1.0, 0.6),
     'L0_xattn_ln2_offset': (0.0, 0.8),
     'L0_xattn_bq2': (0.0, 0.8),
     'L0_xattn_bk2': (0.0, 2.0),
     'L0_xattn_bv2': (0.0, 0.1),
     'L0_xattn_bo2': (0.0, 0.1),
     'L0_xattn_ln_mlp_scale': (1.0, 0.6),
     'L0_xattn_ln_mlp_offset': (0.0, 0.697),
     'L0_xattn_b_fc1': (0.0, 0.1),
     'L0_xattn_b_fc2': (0.0, 0.1),
     'L1_xattn_ln1_w': (1.0, 0.6),
     'L1_xattn_ln1_b': (0.0, 0.8),
     'L1_xattn_q_b': (0.0, 0.8),
     'L1_xattn_k_b': (0.0, 2.0),
     'L1_xattn_v_b': (0.0, 0.287),
     'L1_xattn_cproj_b': (0.0, 0.1),
     'L1_xattn_ln2_w': (1.0, 0.6),
     'L1_xattn_ln2_b': (0.0, 0.8),
     'L1_xattn_fc_b': (0.0, 0.1),
     'L1_xattn_proj_b': (0.0, 0.1),
     'L2_xattn_q_b': (0.0, 2.0),
     'L2_xattn_kv_b': (0.0, 0.8),
     'L2_xattn_out_b': (0.0, 2.0),
     'L2_xattn_postnorm_w': (1.0, 0.6),
     'L2_xattn_mlp_b1': (0.0, 0.1),
     'L2_xattn_mlp_b2': (0.0, 0.1),
     'L3_xattn_bq': (0.0, 0.8),
     'L3_xattn_bk': (0.0, 2.0),
     'L3_xattn_bv': (0.0, 0.294),
     'L3_xattn_bo': (0.0, 0.1),
     'L3_xattn_gamma': (1.0, 0.2),
     'L3_xattn_beta': (0.0, 0.1)}
    factors = {'L0_xattn_wq1': 8.0,
     'L0_xattn_wk1': 8.0,
     'L0_xattn_bias_k1': 64.0,
     'L0_xattn_bias_v1': 64.0,
     'L0_xattn_wq2': 8.0,
     'L0_xattn_wk2': 8.0,
     'L0_xattn_bias_k2': 64.0,
     'L0_xattn_bias_v2': 64.0,
     'L1_xattn_q_w': 8.0,
     'L1_xattn_k_w': 8.0,
     'L2_xattn_q_w': 8.0,
     'L2_xattn_kv_w': 8.0,
     'L2_xattn_out_w': 8.0,
     'L3_xattn_Wq': 8.0,
     'L3_xattn_Wk': 8.0}
    for name, (base, spread) in spreads.items():
        noise = np.random.default_rng([zlib.crc32(name.encode()), seed]).standard_normal(out[name].shape)
        drawn = base * np.exp(spread * noise) if base else spread * noise
        out[name] = jnp.asarray(drawn.astype(out[name].dtype))
    for name, factor in factors.items():
        out[name] = (out[name] * factor).astype(out[name].dtype)
    return out
```

```python
from contextlib import ExitStack

import concourse.bass as bass
from concourse import mybir

F32 = mybir.dt.float32
F32R = mybir.dt.float32r
BF16 = mybir.dt.bfloat16
ALU = mybir.AluOpType
ACT = mybir.ActivationFunctionType
AX = mybir.AxisListType

NB = 4
TOK = 256
CH = 2048
NSLOT = 8


class Ctx:

    def __init__(self, nc, stack):
        self.nc, self.stack = nc, stack
        self.sems, self.n, self.seen, self.last = {}, {}, {}, {}
        self.id = 0

    def sem(self, role):
        if role not in self.sems:
            self.sems[role] = self.stack.enter_context(self.nc.semaphore("s_" + role))
            self.n[role] = 0
        return self.sems[role]

    def sig(self, ins, role, by=1):
        s = self.sem(role)
        ins.then_inc(s, by)
        self.n[role] += by
        self.last[role if by == 16 else role.split("_")[0]] = (role, self.n[role])
        return (role, self.n[role])

    def wait(self, eng, *marks):
        for m in marks:
            if m is None:
                continue
            key = (id(eng), m[0])
            if self.seen.get(key, 0) < m[1]:
                eng.wait_ge(self.sems[m[0]], m[1])
                self.seen[key] = m[1]

    def sb(self, stack, name, shape, dt=F32):
        self.id += 1
        return stack.enter_context(self.nc.sbuf_tensor(f"{name}_{self.id}", shape, dt))


def f32(ap):
    return ap.bitcast(F32)


COLS = {}


def _cols():
    at = 0
    for a in range(2):
        for name, n in (("ln_s", 2), ("ln_o", 2), ("bq", 16), ("bk", 16), ("bv", 16),
                        ("bias_k", 16), ("bias_v", 16)):
            COLS[name, a] = (at, n)
            at += n
    for m in range(3):
        for name, n in (("m_s", 2), ("m_o", 2), ("m_b1", 8)):
            COLS[name, m] = (at, n)
            at += n
    for name, n in (("l_s", 2), ("l_o", 2)):
        COLS[name, 1] = (at, n)
        at += n
    for l in (1, 2, 3):
        for name, n in (("qb", 2), ("kb", 2)):
            COLS[name, l] = (at, n)
            at += n
    return at


NCOL = _cols()
ROWS = {n: i for i, n in enumerate(("bo0", "bo1", "b2_0", "vb1", "ob1", "b2_1", "vb2", "ob2", "b2_2",
                                    "vb3", "ob3", "gamma", "beta"))}
NROW = len(ROWS)
QSCALE = {18: 0.25, 21: 1.0 / 16.0, 24: 8.0 ** -0.5}
CHUNK = {"mlp0a": 16, "mlp0b": 17, "proj1": 18, "mlp1a": 19, "mlp1b": 20, "proj2": 21,
         "mlp2a": 22, "mlp2b": 23, "proj3": 24}
SLOT = {"mlp0a": 0, "mlp0b": 1, "proj1": 2, "mlp1a": 3, "mlp1b": 4, "proj2": 5,
        "mlp2a": 6, "mlp2b": 7, "proj3": 0}


def program(nc, x_in, ctx_in, mask1, mask2, mask3, wts, cols_in, rows_in, ident_in, out, upto=9):
    with ExitStack() as top:
        k = Ctx(nc, top)
        pe, act, dve, pool, sp = nc.tensor, nc.scalar, nc.vector, nc.gpsimd, nc.sync
        sig, wait = k.sig, k.wait

        Wt = {}

        def slots(stack, names):
            for n in names:
                Wt[n] = k.sb(stack, f"W{n}x", [128, 2 * CH], F32R)

        slots(top, (5,))
        CTh = k.sb(top, "CTh", [128, 2, NB * TOK], F32R)
        CTl = k.sb(top, "CTl", [128, 2, NB * TOK], F32R)
        X = k.sb(top, "X", [128, NB * 2, 256])
        ident = k.sb(top, "ident", [128, 128])
        cols = k.sb(top, "cols", [128, NCOL])
        small = k.sb(top, "small", [128, 64])
        neghalf = small[:, 60:62]
        stage = k.sb(top, "stage", [128, 4, 512])
        B = [top.enter_context(nc.psum_tensor(f"bank{i}", [128, 512], F32)) for i in range(8)]

        def col(name, i, j=0, n=1):
            at = COLS[name, i][0] + j
            return cols[:, at:at + n]

        ld_id = sig(sp.dma_start(ident[:], ident_in), "ld_id", 16)
        ld_cols = sig(sp.dma_start(cols[:], cols_in), "ld_cols", 16)
        ld_x = [None] * NB

        def load_x(b):
            ld_x[b] = sig(sp.dma_start(X[:, 2 * b:2 * b + 2, :], x_in[b].rearrange("(t p) d -> p t d", p=128)),
                          f"ld_x{b}", 16)

        def all_wait(*marks):
            for e in (pe, act, dve, pool, sp):
                wait(e, *marks)

        nh = sig(dve.memset(neghalf, -0.5), "nh")

        chunks = {}

        def make_loader(stage, nst, tag):
            state = {"n": 0, "free": [None] * nst}

            def load(c, j):
                r = state["n"] % nst
                state["n"] += 1
                wait(sp, *(state["free"][r] or ()))
                mark = sig(sp.dma_start(stage[:, r, :], wts[c][:, 512 * j:512 * j + 512]), f"ld_w{tag}{r}", 16)
                return r, mark

            def pieces(c, slot, scale, ncol, free):
                done = chunks[c] = {"marks": []}

                def piece(j, r, mark):
                    src = stage[:, r, :]
                    hi = Wt[slot][:, 512 * j:512 * j + 512]
                    lo = Wt[slot][:, CH + 512 * j:CH + 512 * j + 512]
                    s = scale if j == 0 else 1.0
                    wait(act, mark, *free())
                    if s != 1.0:
                        h = sig(act.activation(hi, src, ACT.Identity, scale=s), "act_whi")
                    else:
                        h = sig(act.copy(hi, src), "act_whi")
                    wait(dve, mark, h)
                    if s != 1.0:
                        l = sig(dve.scalar_tensor_tensor(out=lo, in0=src, scalar=s, in1=f32(hi),
                                                         op0=ALU.mult, op1=ALU.subtract), "dve_wlo")
                    else:
                        l = sig(dve.tensor_tensor(lo, src, f32(hi), ALU.subtract), "dve_wlo")
                    done["marks"] = [h, l]
                    state["free"][r] = (h, l)
                return [(lambda j=j: load(c, j), lambda r, m, j=j: piece(j, r, m)) for j in range(ncol)]
            pieces.state = state
            return pieces

        pieces = make_loader(stage, 4, "a")
        queue, loaded = [], []

        def pop(n):
            for _ in range(n):
                if loaded:
                    mark, split = loaded.pop(0)
                    split(*mark)
            while queue and len(loaded) < 4:
                load, split = queue.pop(0)
                loaded.append((load(), split))

        def boundary():
            all_wait(*k.last.values())

        def ln_stats(b, src, eps, rms, need, scr, tag):
            st, mv, rs, xn = scr["st"], scr["mv"], scr["rs"], scr["xn"]
            wait(dve, *need)
            wait(dve, *scr.get("xn_free", ()), *scr.get("st_free", ()))
            for t in range(2):
                m = sig(dve.bn_stats(st[:, t, :], src[:, t, :]), "dve_bn")
            wait(dve, m)
            for t in range(2):
                m = sig(dve.bn_aggr(mv[:, t, :], st[:, t, :]), "dve_bn")
            scr["st_free"] = (m,)
            if rms:
                wait(dve, m)
                m = sig(dve.tensor_tensor(rs[:, 0:2], mv[:, :, 0], mv[:, :, 0], ALU.mult), "dve_bn")
                wait(dve, m)
                m = sig(dve.tensor_tensor(mv[:, :, 1], mv[:, :, 1], rs[:, 0:2], ALU.add), "dve_bn")
            wait(pool, m, nh)
            m = sig(pool.tensor_scalar(rs[:, 2:4], mv[:, :, 1], eps, None, ALU.add), "pool_ln")
            wait(pool, m)
            m = sig(pool.tensor_tensor(rs[:, 4:6], rs[:, 2:4], neghalf, ALU.pow), "pool_ln")
            wait(dve, m)
            for t in range(2):
                if rms:
                    m = sig(dve.tensor_scalar(xn[:, t, :], src[:, t, :], rs[:, 4 + t:5 + t], None,
                                              ALU.mult), "dve_xn")
                else:
                    m = sig(dve.tensor_scalar(xn[:, t, :], src[:, t, :], mv[:, t, 0:1],
                                              rs[:, 4 + t:5 + t], ALU.subtract, ALU.mult), "dve_xn")
            return m

        def ln_turn(xn_mark, bank, bank_free, dst_h, dst_l, dst_free, s_col, o_col, scr):
            wait(pe, xn_mark, bank_free, ld_id)
            xn = hf = scr["xn"]
            for d in range(2):
                for t in range(2):
                    m = pe.transpose(bank[:, d * 256 + t * 128:d * 256 + t * 128 + 128],
                                     xn[:, t, d * 128:d * 128 + 128], ident[:])
            m = sig(m, "pe_lnT")
            wait(dve, m, ld_cols)
            for d in range(2):
                src = bank[:, d * 256:d * 256 + 256]
                if o_col is None:
                    m = sig(dve.tensor_scalar(hf[:, d, :], src, s_col(d), None, ALU.mult), "dve_hf")
                else:
                    m = sig(dve.tensor_scalar(hf[:, d, :], src, s_col(d), o_col(d), ALU.mult, ALU.add),
                            "dve_hf")
            done = m
            wait(act, m, *dst_free)
            h = sig(act.copy(dst_h, hf[:]), "act_hhi")
            wait(dve, h)
            l = sig(dve.tensor_tensor(dst_l, hf[:], f32(dst_h), ALU.subtract), "dve_hlo")
            scr["xn_free"] = (l,)
            return done, (h, l)

        def ln_scratch(st, n=""):
            return {"st": k.sb(st, "bnst", [128, 2, 6]), "mv": k.sb(st, "bnmv", [128, 2, 2]),
                    "rs": k.sb(st, "bnrs", [128, 6]), "xn": k.sb(st, "xn", [128, 2, 256])}

        def mm3(o, wh, wl, xh, xl, first, last, skip=False):
            pe.matmul(o, wh, xh, start=first, stop=False, skip_group_check=skip)
            pe.matmul(o, wh, xl, start=False, stop=False, skip_group_check=skip)
            return pe.matmul(o, wl, xh, start=False, stop=last, skip_group_check=skip)

        x_done = [None] * NB

        early = top.enter_context(ExitStack())
        slots(early, (2, 3, 4))
        earlier = early.enter_context(ExitStack())
        slots(earlier, (0, 1, 6, 7))
        with ExitStack() as st:
            QTh = k.sb(st, "QTh", [128, 2, 256], F32R)
            QTl = k.sb(st, "QTl", [128, 2, 256], F32R)
            KT = k.sb(st, "KT", [128, 2, 2, 258], F32R)
            Vh = k.sb(st, "Vh", [128, 2, 2, 256], F32R)
            Vl = k.sb(st, "Vl", [128, 2, 2, 256], F32R)
            E = k.sb(st, "E", [128, 3, 2, 258])
            PTh = k.sb(st, "PTh", [128, 2, 256], F32R)
            PTl = k.sb(st, "PTl", [128, 2, 256], F32R)
            OTh = k.sb(st, "OTh", [128, 256], F32R)
            OTl = k.sb(st, "OTl", [128, 256], F32R)
            hTh = k.sb(st, "hTh", [128, 2, 2, 256], F32R)
            hTl = k.sb(st, "hTl", [128, 2, 2, 256], F32R)
            nm = k.sb(st, "nm", [128, 4, 2])
            ls = k.sb(st, "ls", [128, 4, 2])
            rl = k.sb(st, "rl", [128, 4, 2])
            pb = k.sb(st, "pb", [128, 2, 2, 32])
            pbT = k.sb(st, "pbT", [128, 256])
            Cst = k.sb(st, "Cst", [128, 256])
            BVh = k.sb(st, "BVh", [128, 400], F32R)
            BVl = k.sb(st, "BVl", [128, 400], F32R)
            BK = k.sb(st, "BK", [128, 16, 2, 2], F32R)
            bqs = k.sb(st, "bqs", [128, 2, 16])
            bo = k.sb(st, "bo", [128, 256])
            scr = ln_scratch(st)
            SC = 1.0 / float(128.0 ** 0.5)
            accB, S0, S1, QKB, VB, PTB, OTB, MISC = B

            ldc, ct = [], []
            for r in range(4):
                ldc.append(sig(sp.dma_start(stage[:, r, :], ctx_in[128 * (r // 2):128 * (r // 2) + 128,
                                                                   512 * (r % 2):512 * (r % 2) + 512]),
                               f"ld_c{r}", 16))
            load_x(0)
            for r in range(4):
                cc = slice(512 * (r % 2), 512 * (r % 2) + 512)
                wait(act, ldc[r])
                h = sig(act.copy(CTh[:, r // 2, cc], stage[:, r, :]), "act_ct")
                wait(dve, ldc[r], h)
                l = sig(dve.tensor_tensor(CTl[:, r // 2, cc], stage[:, r, :], f32(CTh[:, r // 2, cc]),
                                          ALU.subtract), "dve_ct")
                ct += [h, l]
                pieces.state["free"][r] = (h, l)

            wait(dve, ld_cols)
            z1 = sig(dve.memset(pb[:], 0.0), "dve_ini")
            wait(dve, z1)
            pb1 = sig(dve.memset(pb[:, :, :, 16:17], 1.0), "dve_ini")
            pbz = sig(dve.memset(pbT[:], 0.0), "dve_ini")
            for a in range(2):
                bqm = sig(dve.tensor_scalar(bqs[:, a, :], col("bq", a, 0, 16), SC, None, ALU.mult), "dve_ini")
            BVf = scr["xn"]

            prep = {}

            def consts(a, bv_free):
                bvf = BVf[:].rearrange("p a b -> p (a b)")[:, 0:400]
                wait(dve, *scr.get("xn_free", ()), *bv_free)
                m = sig(dve.memset(bvf, 0.0), "dve_bv")
                wait(dve, m, ld_cols)
                m = sig(dve.tensor_tensor(bvf[:, 0:18 * 15 + 1:18], col("bias_v", a, 0, 16),
                                          col("bv", a, 0, 16), ALU.subtract), "dve_bv")
                m = sig(dve.tensor_copy(bvf[:, 16:16 + 17 * 15 + 1:17], col("bv", a, 0, 16)), "dve_bv")
                wait(dve, m)
                m = sig(dve.tensor_copy(BVh[:], bvf), "dve_bv")
                wait(dve, m)
                m = sig(dve.tensor_tensor(BVl[:], bvf, f32(BVh[:]), ALU.subtract), "dve_bv")
                scr["xn_free"] = (m,)
                prep["bv", a] = m

            def key_biases(a, bk_free):
                wait(dve, *bk_free)
                if a == 0:
                    m = sig(dve.memset(f32(BK[:]), 0.0), "dve_bk")
                    wait(dve, m)
                m = sig(dve.tensor_copy(BK[:, :, 0, 0], col("bias_k", a, 0, 16)), "dve_bk")
                wait(dve, m)
                prep["bk", a] = sig(dve.tensor_tensor(BK[:, :, 1, 0], col("bias_k", a, 0, 16),
                                                      f32(BK[:, :, 0, 0]), ALU.subtract), "dve_bk")

            def load_bo(a):
                wait(sp, *prep.get("bo_free", ()))
                prep["bo", a] = sig(sp.dma_start(bo[:], rows_in[ROWS[f"bo{a}"]]), "ld_bo", 16)

            NI = 128
            T = {}

            def g(name, i):
                return T.get((name, i))

            def dec(i):
                return i // 64, (i // 16) % 4, i % 16

            def prelude(a, b):
                n = a * 4 + b
                need = (ld_x[b],) if a == 0 else (x_done[b],)
                T["ln", n] = ln_stats(b, X[:, 2 * b:2 * b + 2, :], 1e-5, False, need, scr, "a")

            def prelude_turn(a, b):
                n = a * 4 + b
                m = T["ln", n]
                free = (g("qk", 16 * (n - 2) + 15),) if n >= 2 else ()
                r, marks = ln_turn(m, MISC, T.get("misc_free"), hTh[:, n % 2], hTl[:, n % 2], free,
                                   lambda d: col("ln_s", a, d), lambda d: col("ln_o", a, d), scr)
                T["misc_free"] = r
                T["hT", n] = marks
                wait(pool, m, prep["bo", a])
                m = pool.tensor_tensor(X[:, 2 * b, :], X[:, 2 * b, :], bo[:], ALU.add)
                T["xb", n] = sig(pool.tensor_tensor(X[:, 2 * b + 1, :], X[:, 2 * b + 1, :], bo[:], ALU.add),
                                 "pool_xb")
                prep["bo_free"] = (T["xb", n],)

            def stA(i):
                a, b, h = dec(i)
                c, p, o = 8 * a + h // 2, h // 2, (h % 2) * 128
                n, j = 4 * a + b, i % 2
                wait(pe, *chunks[c]["marks"], *T["hT", n], *ct, g("qk_lo", i - 1))
                for d in range(2):
                    ws = Wt[p][:, d * 256 + o:d * 256 + o + 128]
                    wl = Wt[p][:, CH + d * 256 + o:CH + d * 256 + o + 128]
                    mm3(QKB[:, 0:256], ws, wl, hTh[:, n % 2, d, :], hTl[:, n % 2, d, :], d == 0, d == 1)
                for d in range(2):
                    ws = Wt[p][:, 512 + d * 256 + o:512 + d * 256 + o + 128]
                    wl = Wt[p][:, CH + 512 + d * 256 + o:CH + 512 + d * 256 + o + 128]
                    m = mm3(QKB[:, 256:512], ws, wl, CTh[:, d, b * 256:b * 256 + 256],
                            CTl[:, d, b * 256:b * 256 + 256], d == 0, d == 1)
                T["qk", i] = sig(m, "pe_qk")

            def stA_ev(i):
                a, b, h = dec(i)
                j = i % 2
                wait(act, T["qk", i], g("s", i - 2), bqm)
                qh = sig(act.activation(QTh[:, j, :], QKB[:, 0:256], ACT.Identity, bias=bqs[:, a, h:h + 1]),
                         "act_qk")
                kh = sig(act.activation(KT[:, j, 0, 0:256], QKB[:, 256:512], ACT.Identity,
                                        bias=col("bk", a, h)), "act_qk")
                wait(dve, T["qk", i], g("s", i - 2), kh)
                dve.scalar_tensor_tensor(out=QTl[:, j, :], in0=QKB[:, 0:256], scalar=bqs[:, a, h:h + 1],
                                         in1=f32(QTh[:, j, :]), op0=ALU.add, op1=ALU.subtract)
                T["qk_lo", i] = sig(dve.scalar_tensor_tensor(
                    out=KT[:, j, 1, 0:256], in0=QKB[:, 256:512], scalar=col("bk", a, h),
                    in1=f32(KT[:, j, 0, 0:256]), op0=ALU.add, op1=ALU.subtract), "dve_qk")

            def key_column(i):
                a, b, h = dec(i)
                j = i % 2
                wait(pool, g("s", i - 2), prep["bk", a])
                T["bk", i] = sig(pool.tensor_copy(KT[:, j, :, 256:258], f32(BK[:, h])), "pool_bk")

            def stV(i):
                a, b, h = dec(i)
                p, j, t = h // 2, (i // 2) % 2, i % 2
                if t == 0:
                    wait(pe, g("v_lo", i - 2))
                for d in range(2):
                    t0 = b * 256 + t * 128
                    m = mm3(VB[:, t * 256:t * 256 + 256], CTh[:, d, t0:t0 + 128], CTl[:, d, t0:t0 + 128],
                            Wt[p][:, 1024 + d * 256:1280 + d * 256],
                            Wt[p][:, CH + 1024 + d * 256:CH + 1280 + d * 256], d == 0, d == 1)
                if t == 1:
                    m = sig(m, "pe_v")
                    wait(act, m, g("o", i - 4))
                    vh = sig(act.copy(Vh[:, j], VB[:]), "act_v")
                    wait(dve, vh, g("o", i - 4))
                    T["v_lo", i - 1] = T["v_lo", i] = sig(
                        dve.tensor_tensor(Vl[:, j], VB[:].rearrange("p (a b) -> p a b", a=2), f32(Vh[:, j]),
                                          ALU.subtract), "dve_v")

            def stB(i):
                a, b, h = dec(i)
                j = i % 2
                wait(pe, T["qk_lo", i], T["bk", i], g("exp", i - 1))
                for t, bank in enumerate((S0, S1)):
                    qs = QTh[:, j, t * 128:t * 128 + 128]
                    ql = QTl[:, j, t * 128:t * 128 + 128]
                    m = mm3(bank[:, 0:258], qs, ql, KT[:, j, 0, :], KT[:, j, 1, :], True, True)
                T["s", i] = sig(m, "pe_s")
                r = i % 4
                wait(dve, T["s", i], g("exp", i - 4))
                for t, bank in enumerate((S0, S1)):
                    m = sig(dve.tensor_reduce(nm[:, r, t:t + 1], bank[:, 0:257], AX.X, ALU.max, negate=True),
                            "dve_max")
                    T["max", i, t] = m

            def stBx(i):
                r = i % 4
                for t, bank in enumerate((S0, S1)):
                    wait(act, T["max", i, t], g("t", i - 3), g("rl", i - 4))
                    m = sig(act.activation(E[:, i % 3, t, 0:257], bank[:, 0:257], ACT.Exp,
                                           bias=nm[:, r, t:t + 1], accum_out=ls[:, r, t:t + 1]), "act_exp")
                T["exp", i] = m

            def stB2(i):
                a, b, h = dec(i)
                r, n = i % 4, i // 16
                wait(dve, T["exp", i], g("pn", i - 4))
                T["rl", i] = sig(dve.reciprocal(rl[:, r, :], ls[:, r, :]), "dve_rl")
                wait(pool, T["rl", i], pb1, g("pbT", n - 2))
                pool.tensor_tensor(pb[:, n % 2, :, h], E[:, i % 3, :, 256], rl[:, r, :], ALU.mult)
                for t in range(2):
                    m = sig(pool.tensor_scalar(E[:, i % 3, t, 0:256], E[:, i % 3, t, 0:256],
                                               rl[:, r, t:t + 1], None, ALU.mult), "pool_pn")
                T["pn", i] = m

            def stC(i):
                wait(pe, T["pn", i], g("pt_lo", i - 1), ld_id)
                for t in range(2):
                    for s in range(2):
                        m = pe.transpose(PTB[:, s * 256 + t * 128:s * 256 + t * 128 + 128],
                                         E[:, i % 3, t, s * 128:s * 128 + 128], ident[:])
                T["t", i] = sig(m, "pe_t")
                wait(act, T["t", i], g("o", i - 1))
                m = sig(act.copy(PTh[:], PTB[:]), "act_pt")
                wait(dve, m, g("o", i - 1))
                T["pt_lo", i] = sig(dve.tensor_tensor(PTl[:], PTB[:].rearrange("p (a b) -> p a b", a=2),
                                                      f32(PTh[:]), ALU.subtract), "dve_pt")

            def stD(i):
                a, b, h = dec(i)
                j, o = (i // 2) % 2, (h % 2) * 128
                wait(pe, T["pt_lo", i], T["v_lo", i], g("ot_lo", i - 1))
                for s in range(2):
                    m = mm3(OTB[:, 0:256], Vh[:, j, s, o:o + 128], Vl[:, j, s, o:o + 128],
                            PTh[:, s, :], PTl[:, s, :], s == 0, s == 1)
                T["o", i] = sig(m, "pe_o")
                wait(act, T["o", i], g("w", i - 1))
                m = sig(act.copy(OTh[:], OTB[:, 0:256]), "act_ot")
                wait(dve, m, g("w", i - 1))
                T["ot_lo", i] = sig(dve.tensor_tensor(OTl[:], OTB[:, 0:256], f32(OTh[:]), ALU.subtract),
                                    "dve_ot")

            def stE(i):
                a, b, h = dec(i)
                n, p = i // 16, h // 2
                wait(pe, T["ot_lo", i])
                if h == 0:
                    wait(pe, g("x", n - 1))
                o = 1536 + (h % 2) * 256
                for t in range(2):
                    m = mm3(accB[:, t * 256:t * 256 + 256], OTh[:, t * 128:t * 128 + 128],
                            OTl[:, t * 128:t * 128 + 128], Wt[p][:, o:o + 256], Wt[p][:, CH + o:CH + o + 256],
                            h == 0 and t == 0, False, skip=True)
                T["w", i] = sig(m, "pe_w")

            def turn_pb(n):
                wait(pe, T["pn", 16 * n + 15], T.get("misc_free"))
                for t in range(2):
                    m = pe.transpose(MISC[0:32, t * 128:t * 128 + 128], pb[:, n % 2, t, :], ident[:])
                T["pbT", n] = m = sig(m, "pe_pbT")
                wait(act, m, g("cc", n - 1), pbz)
                T["misc_free"] = T["pbTs", n] = sig(act.copy(pbT[0:32, :], MISC[0:32, 0:256]),
                                                            "act_pbT")

            def close(n):
                wait(pe, T["pbTs", n], T["cst", n // 4])
                for t in range(2):
                    m = pe.matmul(accB[:, t * 256:t * 256 + 256], pbT[:, t * 128:t * 128 + 128], Cst[:],
                                  start=False, stop=True, skip_group_check=True)
                T["cc", n] = sig(m, "pe_cc")
                b = n % 4
                wait(dve, T["cc", n], T["xb", n])
                T["x", n] = x_done[b] = sig(dve.tensor_tensor(
                    X[:, 2 * b:2 * b + 2, :], accB[:].rearrange("p (a b) -> p a b", a=2),
                    X[:, 2 * b:2 * b + 2, :], ALU.add), "dve_x")

            def value_biases(a):
                wait(pe, prep["bv", a], T.get("misc_free"), *chunks[8 * a + 7]["marks"])
                for h in range(16):
                    o = 1536 + (h % 2) * 256
                    m = mm3(MISC[:, 0:256], BVh[:, 17 * h:17 * h + 128], BVl[:, 17 * h:17 * h + 128],
                            Wt[h // 2][:, o:o + 256], Wt[h // 2][:, CH + o:CH + o + 256], h == 0, h == 15)
                T["bvmm", a] = m = sig(m, "pe_cst")
                wait(act, m, g("cc", 4 * a - 1))
                T["misc_free"] = T["cst", a] = sig(act.copy(Cst[:], MISC[:, 0:256]), "act_cst")

            consts(0, ())
            key_biases(0, ())
            load_bo(0)
            queue += pieces(0, 0, SC, 4, lambda: ())
            pop(0)
            prelude(0, 0)
            prelude_turn(0, 0)
            queue += pieces(1, 1, SC, 4, lambda: ())
            for b in range(1, NB):
                load_x(b)
            pop(4)
            pop(2)
            stA(0)
            stA_ev(0)
            key_column(0)
            for t in range(NI + 4):
                if t < 12 and t % 2 == 0:
                    queue += pieces(2 + t // 2, 2 + t // 2, SC, 4, lambda: ())
                u = t - 54
                if u >= 0 and u % 2 == 0 and u // 2 < 8:
                    p = u // 2
                    queue += pieces(8 + p, p, SC, 4, lambda p=p: (T["w", 48 + 2 * p + 1],
                                                                      T["bvmm", 0]))
                if t + 1 < NI:
                    key_column(t + 1)
                u = t - 118
                if u >= 0 and u % 2 == 0 and u // 2 < 6:
                    p = u // 2
                    queue += pieces(16 + p, p, QSCALE.get(16 + p, 1.0), 4,
                                    lambda p=p: (T["w", 112 + 2 * p + 1], T["bvmm", 1]))
                if t < NI:
                    stB(t)
                    stBx(t)
                    stB2(t)
                if t + 1 < NI:
                    stA(t + 1)
                    stA_ev(t + 1)
                if t < NI:
                    stV(t)
                if t >= 4:
                    stE(t - 4)
                    if (t - 4) % 16 == 15:
                        close((t - 4) // 16)
                    if (t - 3) % 16 == 15:
                        turn_pb((t - 3) // 16)
                if 3 <= t < NI + 3:
                    stD(t - 3)
                if 2 <= t < NI + 2:
                    stC(t - 2)
                pop(2)
                if t == 50:
                    consts(1, (T["bvmm", 0],))
                    load_bo(1)
                if t % 16 == 8 and t // 16 < 7:
                    prelude((t // 16 + 1) // 4, (t // 16 + 1) % 4)
                if t % 16 == 11 and t // 16 < 7:
                    prelude_turn((t // 16 + 1) // 4, (t // 16 + 1) % 4)
                if t % 64 == 13:
                    value_biases(t // 64)
                if t == 62:
                    key_biases(1, (T["bk", 63],))
            for p in range((NI + 4 - 118 + 1) // 2, 6):
                queue += pieces(16 + p, p, QSCALE.get(16 + p, 1.0), 4, lambda: (T["w", NI - 1],))
            boundary()

        def finish(src, *marks):
            wait(sp, *marks)
            fin = sig(sp.dma_start(out.rearrange("b (t p) d -> p (b t) d", p=128), src), "st", 16)
            wait(sp, fin)

        if upto == 0:
            finish(X[:], *x_done)
            return

        def mlp(m, gelu, wa, wb, row, src, rms, src_done):
            with ExitStack() as st:
                hTh = k.sb(st, "mhTh", [128, 2, 2, 512], F32R)
                hTl = k.sb(st, "mhTl", [128, 2, 2, 512], F32R)
                G = k.sb(st, "G", [128, 2, 512])
                GH = k.sb(st, "GH", [128, 2, 512], F32R)
                GL = k.sb(st, "GL", [128, 2, 512], F32R)
                b2 = k.sb(st, "b2", [128, 256])
                scr = ln_scratch(st)
                F = B[0:2]
                A2 = [B[2:4], B[4:6]]
                M = [B[6], B[7]]
                T = {}
                b2m = sig(sp.dma_start(b2[:], rows_in[row]), "ld_b2", 16)

                def stats(b):
                    T["xn", b] = ln_stats(b, src[:, 2 * b:2 * b + 2, :], 1e-6 if rms else 1e-5, rms,
                                          (src_done[b],), scr, "m")
                    wait(pool, T["xn", b], b2m, x_done[b])
                    for t in range(2):
                        z = sig(pool.tensor_tensor(X[:, 2 * b + t, :], X[:, 2 * b + t, :], b2[:], ALU.add),
                                "pool_xb")
                    T["xb", b] = z

                def turn(b):
                    g, o = b // 2, (b % 2) * 256
                    T["mf", b], T["hT", b] = ln_turn(
                        T["xn", b], M[b % 2], T.get(("mf", b - 2)), hTh[:, g, :, o:o + 256],
                        hTl[:, g, :, o:o + 256], (), lambda d: col("m_s", m, d),
                        None if rms else (lambda d: col("m_o", m, d)), scr)

                def fc1(i):
                    g, f = i // 8, i % 8
                    wait(pe, *chunks[16 + wa]["marks"], *T["hT", 2 * g], *T["hT", 2 * g + 1],
                         T.get(("gelu", i - 2)))
                    for d in range(2):
                        o = d * 1024 + f * 128
                        z = mm3(F[i % 2][:], Wt[wa][:, o:o + 128], Wt[wa][:, CH + o:CH + o + 128],
                                hTh[:, g, d, :], hTl[:, g, d, :], d == 0, d == 1)
                    z = sig(z, "pe_f1")
                    wait(act, z, T.get(("gl", i - 2)))
                    T["gelu", i] = z = sig(act.activation(G[:, i % 2, :], F[i % 2][:], gelu,
                                                          bias=col("m_b1", m, f)), "act_gelu")
                    wait(dve, z, T.get(("f2", i - 2)))
                    z = sig(dve.tensor_copy(GH[:, i % 2, :], G[:, i % 2, :]), "dve_gh")
                    wait(dve, z)
                    T["gl", i] = sig(dve.tensor_tensor(GL[:, i % 2, :], G[:, i % 2, :],
                                                       f32(GH[:, i % 2, :]), ALU.subtract), "dve_gl")

                def fc2(i):
                    g, f = i // 8, i % 8
                    wait(pe, T["gl", i], *chunks[16 + wb]["marks"])
                    for t in range(4):
                        z = mm3(A2[g][t // 2][:, (t % 2) * 256:(t % 2) * 256 + 256],
                                GH[:, i % 2, t * 128:t * 128 + 128], GL[:, i % 2, t * 128:t * 128 + 128],
                                Wt[wb][:, f * 256:f * 256 + 256], Wt[wb][:, CH + f * 256:CH + f * 256 + 256],
                                f == 0 and t % 2 == 0, f == 7, skip=True)
                    T["f2", i] = sig(z, "pe_f2")
                    if f == 7:
                        for b in (2 * g, 2 * g + 1):
                            wait(dve, T["f2", i], T["xb", b])
                            x_done[b] = sig(dve.tensor_tensor(
                                X[:, 2 * b:2 * b + 2, :], A2[g][b % 2][:].rearrange("p (a b) -> p a b", a=2),
                                X[:, 2 * b:2 * b + 2, :], ALU.add), "dve_x")

                for b in range(2):
                    stats(b)
                    turn(b)
                pop(4)
                for i in range(17):
                    if i < 16:
                        fc1(i)
                    if i in (2, 4):
                        stats(2 + (i - 2) // 2)
                    if i in (3, 5):
                        turn(2 + (i - 3) // 2)
                    pop(1)
                    if i >= 1:
                        fc2(i - 1)
                pop(12)
                boundary()

        pop(12)
        mlp(0, ACT.Gelu, 0, 1, ROWS["b2_0"], X, False, x_done)
        earlier.close()
        if upto == 1:
            finish(X[:], *x_done)
            return
        def heads(l, sl, mask_in):
            nh, d, nkv = {1: (16, 16, 16), 2: (16, 16, 16), 3: (32, 8, 8)}[l]
            nkt = 4 if l == 2 else 2
            NK = 128 * nkt
            qp, kp = (((0, 0, 0, 1, 1, 1, 2, 2, 2), (0, 1, 2, 0, 1, 2, 0, 1, 2)) if l == 3 else
                      ((0, 0, 1, 1, 0, 2), (0, 1, 0, 1, 2, 0)))
            npr = len(qp)
            R = npr * d + (0 if l == 3 else 1)
            rep_h = nh // nkv
            nm_t = 2 if l != 3 else 1
            c = 16 + {1: 2, 2: 5, 3: 8}[l]
            w = Wt[sl]
            BIG = -3.0e38
            Y = X
            with ExitStack() as st:
                if l == 2:
                    Y = k.sb(late, "Y", [128, 8, 256])
                nb = 2 if l != 2 else 1
                Q = k.sb(st, "Q", [128, 2, nh, 256], BF16)
                K = k.sb(st, "K", [128, 2, nkv, NK], BF16)
                V = k.sb(st, "V", [128, 2, nkt, nkv, 32])
                qP = k.sb(st, "qP", [128, 3, 2, 256], BF16)
                kP = k.sb(st, "kP", [128, 3, 2, 256], BF16)
                qF = k.sb(st, "qF", [128, 2, 256])
                kF = k.sb(st, "kF", [128, 2, 256]) if l != 2 else qF
                NPT = 5 if l == 2 else 6
                hTh = k.sb(st, "hTh", [128, 2, 256], F32R)
                hTl = k.sb(st, "hTl", [128, 2, 256], F32R)
                E = k.sb(st, "E", [128, 3, 2, NK])
                PT = k.sb(st, "PT", [128, NPT, nkt, 256])
                nm = k.sb(st, "nm", [128, 4, 2])
                OS = k.sb(st, "OS", [128, 2, nh // 4, 256])
                On = k.sb(st, "On", [128, 2, 256])
                rl = k.sb(st, "rl", [128, 2, nh])
                OTh = k.sb(st, "OTh", [128, 2, 256], F32R)
                OTl = k.sb(st, "OTl", [128, 2, 256], F32R)
                vb = k.sb(st, "vb", [128, 256])
                ob = k.sb(st, "ob", [128, 256])
                qbs = k.sb(st, "qbs", [128, 2])
                scr = ln_scratch(st)
                SB, PTB, OB, PB, MB = B[0:2], B[2:4], B[4], B[5:7], B[7]
                T = {}
                ldv = sig(sp.dma_start(vb[:], rows_in[ROWS[f"vb{l}"]]), "ld_vb", 16)
                ldo = sig(sp.dma_start(ob[:], rows_in[ROWS[f"ob{l}"]]), "ld_ob", 16)
                if l == 3:
                    gam = k.sb(st, "gam", [128, 256])
                    bet = k.sb(st, "bet", [128, 256])
                    M3 = k.sb(st, "M3", [128, 2, 2, 256])
                    Em = k.sb(st, "Em", [128, 3, 2, 256])
                    Yo = k.sb(st, "Yo", [128, 2, 2, 256])
                    mvo = k.sb(st, "mvo", [128, 2, 8])
                    ldg = sig(sp.dma_start(gam[:], rows_in[ROWS["gamma"]]), "ld_g", 16)
                    ldb = sig(sp.dma_start(bet[:], rows_in[ROWS["beta"]]), "ld_b", 16)
                else:
                    mraw = k.sb(st, "mraw", [128, 2, 256], mask_in.dtype)
                    mrep = k.sb(st, "mrep", [128, 2, 256])
                    mrow = k.sb(st, "mrow", [128, 2, NK], BF16)
                qbm = sig(dve.tensor_scalar(qbs[:], col("qb", l, 0, 2), QSCALE[c], None, ALU.mult), "dve_ini")
                ones = []
                for j in range(2):
                    for t in range(nkt):
                        vinit = sig(pool.memset(V[:, j, t], 1.0), "pool_ini")
                if l != 3:
                    onesr = k.sb(st, "onesr", [128, 256], BF16)
                    z = sig(pool.memset(onesr[:], 1.0), "pool_ini")
                    if l == 2:
                        zr = sig(pool.memset(mrow[:], 0.0), "pool_ini")
                    wait(sp, z)
                    for j in range(2):
                        ones.append(sig(sp.dma_start(Q[96:97, j, :, :], onesr[0:nh, :]), f"ld_one{j}", 16))

                def parts(srcs, P_, Fr, free, tag):
                    marks = []
                    wait(dve, T.get(("F", id(Fr))))
                    for (o, rows, ps, bias, mul) in srcs:
                        if mul is not None:
                            wait(dve, *free)
                            z = sig(dve.scalar_tensor_tensor(out=Fr[0:rows, o, :], in0=ps, scalar=bias,
                                                             in1=mul, op0=ALU.add, op1=ALU.mult), "dve_f" + tag)
                        else:
                            wait(dve, *free)
                            z = sig(dve.tensor_scalar(Fr[0:rows, o, :], ps, bias, None, ALU.add), "dve_f" + tag)
                        marks.append(z)
                    rows, no = srcs[0][1], len(srcs)
                    F_, H_, M_, L_ = Fr[0:rows, 0:no, :], P_[0:rows, 0, 0:no], P_[0:rows, 1, 0:no], P_[0:rows, 2, 0:no]
                    done = marks[-1]
                    wait(act, done, *free)
                    z = sig(act.copy(H_, F_), "act_h" + tag)
                    wait(pool, z)
                    z = sig(pool.tensor_tensor(F_, F_, H_, ALU.subtract), "pool_r" + tag)
                    wait(act, z)
                    z = sig(act.copy(M_, F_), "act_m" + tag)
                    wait(pool, z)
                    z = sig(pool.tensor_tensor(L_, F_, M_, ALU.subtract), "pool_l" + tag)
                    T["F", id(Fr)] = z
                    return done, z

                def scatter(dst, P_, sel, hp, no, marks, dma, free):
                    wait(sp, *marks, *free)
                    out_ = []
                    for n, part in enumerate(sel):
                        for o in range(no):
                            out_.append(sig(sp.dma_start(dst(n, o), P_[0:hp * d, part, o, :]), f"{dma}{n}_{o}", 16))
                    return out_

                def prep_x(b):
                    xb_ = X[:, 2 * b:2 * b + 2, :]
                    if l == 1:
                        T["xn", b] = ln_stats(b, xb_, 1e-5, False, (x_done[b],), scr, "h")
                        m = T["xn", b]
                    wait(pool, ldo, x_done[b])
                    if l == 1:
                        wait(pool, m)

                def prep_turn(b):
                    xb_ = X[:, 2 * b:2 * b + 2, :]
                    free = T.get(("vq", b - 1), ())
                    if l == 1:
                        T["mb"], T["hT", b] = ln_turn(T["xn", b], MB, T.get("mb"), hTh[:], hTl[:], free,
                                                      lambda i: col("l_s", 1, i), lambda i: col("l_o", 1, i), scr)
                        rd = T["xn", b]
                    else:
                        wait(pe, x_done[b], T.get("mb"), ld_id)
                        for e in range(2):
                            for t in range(2):
                                z = pe.transpose(MB[:, e * 256 + t * 128:e * 256 + t * 128 + 128],
                                                 X[:, 2 * b + t, e * 128:e * 128 + 128], ident[:])
                        rd = z = sig(z, "pe_xT")
                        wait(act, z, *free)
                        h = sig(act.copy(hTh[:], MB[:]), "act_hhi")
                        wait(dve, h, *free)
                        lo = sig(dve.tensor_tensor(hTl[:], MB[:].rearrange("p (a b) -> p a b", a=2), f32(hTh[:]),
                                                   ALU.subtract), "dve_hlo")
                        T["mb"] = lo
                        T["hT", b] = (h, lo)
                    wait(pool, rd, ldo, x_done[b])
                    for t in range(2):
                        z = sig(pool.tensor_tensor(Y[:, 2 * b + t, :], X[:, 2 * b + t, :], ob[:], ALU.add), "pool_xb")
                    T["xb", b] = z

                def prep_q(b):
                    j = b % 2
                    ps = PB[0]
                    wait(pe, *T["hT", b], *chunks[c]["marks"], T.get("pb0"))
                    for m in range(2):
                        for e in range(2):
                            o = e * 256 + m * 128
                            z = mm3(ps[:, m * 256:m * 256 + 256], w[:, o:o + 128], w[:, CH + o:CH + o + 128],
                                    hTh[:, e, :], hTl[:, e, :], e == 0, e == 1)
                    z = sig(z, "pe_q")
                    T["qmm", b] = z
                    srcs = [(m, 128, ps[:, m * 256:m * 256 + 256], qbs[:, m:m + 1], None) for m in range(2)]
                    T["pb0"], z = parts(srcs, qP, qF, (z, qbm, *T.get("qdma", ())), "q")
                    hp = 128 // d
                    T["qdma"] = scatter(lambda n, o: Q[n * d:n * d + d, j, o * hp:o * hp + hp, :], qP, qp, hp, 2,
                                        (z,), "dq", (T.get(("S", b - 2)),))
                    T["Q", b] = list(T["qdma"])

                def prep_mask(b):
                    j = b % 2
                    if l == 3:
                        wait(sp, T.get(("mx", (b - 1) * nh - 1, 1)))
                        T["mask", b] = sig(sp.dma_start(M3[:, j], mask_in[b].rearrange("(t p) s -> p t s", p=128)),
                                           f"ld_m{j}", 16)
                        return
                    wait(sp, T.get(("mrep", b - 2)))
                    z = sig(sp.dma_start(mraw[:, j, :], mask_in[b]), f"ld_m{j}", 16)
                    wait(dve, z, T.get(("kmul", b - 2)), *T.get(("mdma", b - 2), ()))
                    z = sig(dve.tensor_scalar(mrep[:, j, :], mraw[:, j, :], 0.0, None, ALU.not_equal), "dve_mk")
                    T["mrep", b] = z
                    wait(dve, z)
                    if l == 2:
                        wait(dve, zr)
                    z = sig(dve.tensor_scalar(mrow[:, j, 0:256], mrep[:, j, :], 1.0, -BIG, ALU.subtract, ALU.mult),
                            "dve_mk")
                    wait(sp, z, T.get(("S", b - 2)))
                    T["mdma", b] = (sig(sp.dma_start(K[96:97, j, :, :], mrow[0:nkv, j, :]), f"dm{j}", 16),)

                def prep_k(b, half):
                    j = b % 2
                    rh, rl_ = ((CTh[:, :, b * 256:b * 256 + 256], CTl[:, :, b * 256:b * 256 + 256]) if half == 0
                               else (hTh[:], hTl[:]))
                    ps = PB[1]
                    wait(pe, *chunks[c]["marks"], T.get("pb1"))
                    if half:
                        wait(pe, *T["hT", b])
                    for m in range(nm_t):
                        for e in range(2):
                            o = 512 + e * 256 + m * 128 if l != 3 else 1024 + e * 64
                            z = mm3(ps[:, m * 256:m * 256 + 256], w[:, o:o + 128], w[:, CH + o:CH + o + 128],
                                    rh[:, e, :], rl_[:, e, :], e == 0, e == 1)
                    z = sig(z, "pe_k")
                    T["kmm", b] = z
                    rows = 128 if l != 3 else 64
                    mul = mrep[:, j, :] if l != 3 and half == 0 else None
                    srcs = [(m, rows, ps[0:rows, m * 256:m * 256 + 256], col("kb", l, m)[0:rows], mul)
                            for m in range(nm_t)]
                    need = (z, T["mrep", b]) if mul is not None else (z,)
                    T["pb1"], z = parts(srcs, kP, kF, (*need, *T.get("kdma", ())), "k")
                    if half == 0:
                        T["kmul", b] = T["pb1"]
                    hp = rows // d
                    T["kdma"] = scatter(lambda n, o: K[n * d:n * d + d, j, o * hp:o * hp + hp,
                                                       half * 256:half * 256 + 256], kP, kp, hp, nm_t,
                                        (z,), f"dk{half}", (T.get(("S", b - 2)),))
                    T["K", b, half] = list(T["kdma"])

                def prep_v(b, half):
                    j = b % 2
                    lh, ll, t0 = (CTh, CTl, b * 256) if half == 0 else (hTh, hTl, 0)
                    ps = PB[half]
                    wd = nkv * d
                    wait(pe, *chunks[c]["marks"], T.get(f"pb{half}"))
                    for t in range(2):
                        for e in range(2):
                            o = 1024 + e * 256 if l != 3 else 1152 + e * 64
                            s = slice(t0 + t * 128, t0 + t * 128 + 128)
                            z = mm3(ps[:, t * 256:t * 256 + wd], lh[:, e, s], ll[:, e, s], w[:, o:o + wd],
                                    w[:, CH + o:CH + o + wd], e == 0, e == 1)
                    z = sig(z, "pe_v")
                    T["vmm", b] = z
                    wait(dve, z, ldv, vinit, T.get(("PV", b - 2)))
                    for t in range(2):
                        z = sig(dve.tensor_tensor(
                            V[:, j, 2 * half + t, :, 0:d],
                            ps[:, t * 256:t * 256 + wd].rearrange("p (h d) -> p h d", d=d),
                            vb[:, 0:wd].rearrange("p (h d) -> p h d", d=d), ALU.add), "dve_v")
                    T[f"pb{half}"] = z
                    T["V", b] = z
                    T["vq", b] = (T["qmm", b], T["vmm", b], T["kmm", b])

                gq = [0]

                def scores(b, h):
                    i, j = b * nh + h, b % 2
                    wait(pe, *T["Q", b], *T["K", b, 0], *ones)
                    if l != 3:
                        wait(pe, *T["mdma", b])
                    if l == 2:
                        wait(pe, *T["K", b, 1])
                    for t in range(2):
                        if l == 2:
                            ps, o = SB[t], 0
                            wait(pe, T.get(("ex", i - 1, t)))
                        else:
                            ps, o = SB[i % 2], t * 256
                            wait(pe, T.get(("ex", i - 2, 1)), T.get(("mx", i - 2, 1)))
                        z = pe.matmul(ps[:, o:o + NK], Q[0:R, j, h, t * 128:t * 128 + 128], K[0:R, j, h // rep_h, :],
                                      start=True, stop=True)
                        if l == 2:
                            T["s", i, t] = sig(z, "pe_s")
                    if l != 2:
                        T["s", i, 0] = T["s", i, 1] = sig(z, "pe_s")
                    T["S", b] = T["s", i, 1]
                    r = i % 4
                    if l == 1:
                        wait(dve, T["s", i, 1], T.get(("ex", i - 4, 1)))
                        z = sig(dve.tensor_reduce(nm[:, r, :], SB[i % 2][:].rearrange("p (a b) -> p a b", a=2),
                                                  AX.X, ALU.max, negate=True), "dve_mx")
                        T["mx", i, 0] = T["mx", i, 1] = z
                    for t in range(2):
                        if l == 2:
                            wait(dve, T["s", i, t], T.get(("ex", i - 4, 1)))
                            T["mx", i, t] = sig(dve.tensor_reduce(nm[:, r, t:t + 1], SB[t][:], AX.X, ALU.max,
                                                                  negate=True), "dve_mx")
                        if l == 3:
                            wait(dve, T["s", i, 1], T["mask", b], T.get(("ex", i - 3, 1)))
                            T["mx", i, t] = sig(dve.tensor_tensor_reduce(
                                out=Em[:, i % 3, t, :], in0=SB[i % 2][:, t * 256:t * 256 + 256], in1=M3[:, j, t, :],
                                scale=-1.0, scalar=3.4e38, op0=ALU.add, op1=ALU.min,
                                accum_out=nm[:, r, t:t + 1]), "dve_mx")

                def exps(b, h):
                    i = b * nh + h
                    r = i % 4
                    for t in range(2):
                        wait(act, T["mx", i, t], T.get(("T", i - 3)))
                        if l == 3:
                            src = Em[:, i % 3, t, :]
                        elif l == 2:
                            src = SB[t][:]
                        else:
                            src = SB[i % 2][:, t * 256:t * 256 + 256]
                        T["ex", i, t] = sig(act.activation(E[:, i % 3, t, :], src, ACT.Exp, bias=nm[:, r, t:t + 1],
                                                           scale=-1.0 if l == 3 else 1.0), "act_ex")

                def turn(b, h):
                    i = b * nh + h
                    wait(pe, T["ex", i, 1])
                    for u in range(nkt // 2):
                        n = i * (nkt // 2) + u
                        bank = PTB[n % 2]
                        wait(pe, T.get(("ev", n - 2)))
                        for t in range(2):
                            for s in range(2):
                                o = (2 * u + s) * 128
                                z = pe.transpose(bank[:, s * 256 + t * 128:s * 256 + t * 128 + 128],
                                                 E[:, i % 3, t, o:o + 128], ident[:])
                        z = sig(z, "pe_T")
                        dst = PT[:, i % NPT, 2 * u:2 * u + 2, :]
                        src = bank[:].rearrange("p (a b) -> p a b", a=2)
                        if n % 2:
                            wait(act, z, T.get(("pv", (i - NPT) // 4)))
                            T["ev", n] = sig(act.copy(dst, src), "act_ev")
                        else:
                            wait(dve, z, T.get(("pv", (i - NPT) // 4)))
                            T["ev", n] = sig(dve.tensor_copy(dst, src), "dve_ev")
                    T["T", i] = z

                def pv(b, g):
                    i0, j = b * nh + 4 * g, b % 2
                    gi = i0 // 4
                    e0 = (i0 + 4) * (nkt // 2)
                    wait(pe, T["V", b], *[T["ev", n] for n in range(i0 * (nkt // 2), e0)], T.get(("os", gi - 1)))
                    for s in range(nkt):
                        for q in range(4):
                            z = pe.matmul(OB[32 * q:32 * q + 32, 0:256], V[:, j, s, (4 * g + q) // rep_h, :],
                                          PT[:, (i0 + q) % NPT, s, :], start=s == 0, stop=s == nkt - 1,
                                          skip_group_check=True)
                    z = T["pv", gi] = T["PV", b] = sig(z, "pe_pv")
                    wait(act, z, T.get(("post", b - 2)))
                    T["os", gi] = T["OS", b] = sig(act.copy(OS[:, j, g, :], OB[:, 0:256]), "act_os")

                def post_a(b, t):
                    j = b % 2
                    ng = nh // 4
                    for u in range(ng // 4):
                        wait(pe, T["OS", b], T.get("mb"))
                        for g in range(4):
                            z = pe.transpose(MB[:, g * 128:g * 128 + 128], OS[:, j, 4 * u + g, t * 128:t * 128 + 128],
                                             ident[:])
                        z = T["post", b] = sig(z, "pe_po")
                        v = MB[:].rearrange("p (h c) -> p h c", c=32)
                        wait(dve, z, T.get(("on", b - 1)))
                        z = sig(dve.reciprocal(rl[:, t, 16 * u:16 * u + 16], v[:, :, d]), "dve_rl")
                        wait(dve, z)
                        z = sig(dve.tensor_tensor(
                            On[:, t, 16 * d * u:16 * d * u + 16 * d].rearrange("p (h d) -> p h d", d=d), v[:, :, 0:d],
                            rl[:, t, 16 * u:16 * u + 16].unsqueeze(2).broadcast_to([128, 16, d]), ALU.mult), "dve_on")
                        T["mb"] = z
                    T["ond", b] = z

                def post_b(b):
                    wait(pe, T["ond", b], T.get("mb"))
                    for e in range(2):
                        for t in range(2):
                            z = pe.transpose(MB[:, e * 256 + t * 128:e * 256 + t * 128 + 128],
                                             On[:, t, e * 128:e * 128 + 128], ident[:])
                    z = T["on", b] = sig(z, "pe_onT")
                    wait(act, z, T.get(("c", b - 1)))
                    h_ = sig(act.copy(OTh[:], MB[:]), "act_oth")
                    wait(dve, h_, T.get(("c", b - 1)))
                    T["mb"] = T["otl", b] = sig(dve.tensor_tensor(
                        OTl[:], MB[:].rearrange("p (a b) -> p a b", a=2), f32(OTh[:]), ALU.subtract), "dve_otl")

                def post_c(b):
                    wait(pe, T["otl", b])
                    oo = 1536 if l != 3 else 512
                    for t in range(2):
                        for e in range(2):
                            o = oo + e * 256
                            z = mm3(MB[:, t * 256:t * 256 + 256], OTh[:, e, t * 128:t * 128 + 128],
                                    OTl[:, e, t * 128:t * 128 + 128], w[:, o:o + 256], w[:, CH + o:CH + o + 256],
                                    e == 0, e == 1)
                    z = T["c", b] = sig(z, "pe_c")
                    wait(dve, z, T["xb", b])
                    T["mb"] = y_done[b] = sig(dve.tensor_tensor(
                        Y[:, 2 * b:2 * b + 2, :], MB[:].rearrange("p (a b) -> p a b", a=2),
                        Y[:, 2 * b:2 * b + 2, :], ALU.add), "dve_y")
                    if l == 3:
                        last_norm(b)

                def last_norm(b):
                    Yb, j = Y[:, 2 * b:2 * b + 2, :], b % 2
                    m = ln_stats(b, Yb, 1e-6, False, (y_done[b],), scr, "o")
                    xn = scr["xn"]
                    wait(pool, m, ldg, ldb, T.get(("sto", b - 2)))
                    for t in range(2):
                        z = sig(pool.tensor_tensor(Yo[:, j, t, :], xn[:, t, :], gam[:], ALU.mult), "pool_g")
                    scr["xn_free"] = (z,)
                    wait(pool, z)
                    for t in range(2):
                        z = sig(pool.tensor_tensor(Yo[:, j, t, :], Yo[:, j, t, :], bet[:], ALU.add), "pool_g")
                    wait(sp, z)
                    T["sto", b] = sig(sp.dma_start(out[b].rearrange("(t p) d -> p t d", p=128), Yo[:, j]),
                                      f"st_o{j}", 16)

                y_done = [None] * NB

                def prep(b):
                    fs = [lambda: prep_mask(b), lambda: prep_x(b), lambda: prep_turn(b), lambda: prep_q(b),
                          lambda: prep_k(b, 0)]
                    if l == 2:
                        fs.append(lambda: prep_k(b, 1))
                    fs.append(lambda: prep_v(b, 0))
                    if l == 2:
                        fs.append(lambda: prep_v(b, 1))
                    return fs

                for f in prep(0):
                    f()
                todo = []
                N = NB * nh
                for i in range(N + 8):
                    b, h = i // nh, i % nh
                    if h == 0 and b + 1 < NB:
                        todo += prep(b + 1)
                    if i < N:
                        scores(b, h)
                    if 0 <= i - 2 < N:
                        turn((i - 2) // nh, (i - 2) % nh)
                    if i < N:
                        exps(b, h)
                    v = i - 3
                    if 0 <= v < N and v % 4 == 3:
                        pv(v // nh, (v % nh) // 4)
                    v = i - 4
                    if v >= 0 and v % nh == nh - 1:
                        q = v // nh
                        post = [lambda q=q: post_a(q, 0), lambda q=q: post_a(q, 1), lambda q=q: post_b(q),
                                lambda q=q: post_c(q)]
                        todo += post
                    if todo and (h % 2 == 1 or l != 3) or i >= N:
                        for _ in range(1 if i < N else len(todo)):
                            if todo:
                                todo.pop(0)()
                    if h % 2 == 0:
                        pop(1)
                while todo:
                    todo.pop(0)()
                pop(12)
                if l == 3:
                    wait(sp, *[T["sto", b] for b in range(NB)])
                else:
                    boundary()
                return y_done, Y

        yd, _ = heads(1, 2, mask1)
        x_done = yd
        if upto == 2:
            finish(X[:], *x_done)
            return
        mlp(1, ACT.Gelu_apprx_tanh, 3, 4, ROWS["b2_1"], X, False, x_done)
        if upto == 3:
            finish(X[:], *x_done)
            return
        early.close()
        late = top.enter_context(ExitStack())
        slots(late, (6,))
        queue += pieces(22, 6, 1.0, 4, lambda: ())
        yd, Y = heads(2, 5, mask2)
        slots(late, (7,))
        queue += pieces(23, 7, 1.0, 4, lambda: ()) + pieces(24, 5, QSCALE[24], 3, lambda: ())
        mlp(2, ACT.Gelu_apprx_tanh, 6, 7, ROWS["b2_2"], Y, True, yd)
        if upto == 4:
            finish(X[:], *x_done)
            return
        late.close()
        heads(3, 5, mask3)


def layouts(i):
    import numpy as np
    A = {n: np.asarray(v) for n, v in i.items()}

    def dt(w):
        return w.reshape(2, 128, -1).transpose(1, 0, 2)

    chunks = []
    for a in (1, 2):
        wq, wk, wv, wo = (A[f"L0_xattn_{n}{a}"] for n in ("wq", "wk", "wv", "wo"))
        for p in range(8):
            parts = [dt(w[:, 256 * p:256 * p + 256]).reshape(128, 512) for w in (wq, wk, wv)]
            parts.append(wo[256 * p:256 * p + 256].reshape(2, 128, 256).transpose(1, 0, 2).reshape(128, 512))
            chunks.append(np.concatenate(parts, 1))

    def mlp(w1, w2):
        return [dt(w1).reshape(128, 2048), w2.reshape(8, 128, 256).transpose(1, 0, 2).reshape(128, 2048)]

    def dh(w, nh, tile):
        d = w.shape[-1] // nh
        hp = tile // d
        s = w.shape[:-1]
        return w.reshape(*s, nh // hp, hp, d).swapaxes(-1, -2).reshape(*s, nh * d)

    chunks += mlp(A["L0_xattn_w_fc1"], A["L0_xattn_w_fc2"])
    chunks.append(np.concatenate([dt(w).reshape(128, 512) for w in (
        dh(A["L1_xattn_q_w"], 16, 128), dh(A["L1_xattn_k_w"], 16, 128), A["L1_xattn_v_w"],
        A["L1_xattn_cproj_w"])], 1))
    chunks += mlp(A["L1_xattn_fc_w"], A["L1_xattn_proj_w"])
    kv = A["L2_xattn_kv_w"]
    chunks.append(np.concatenate([dt(w).reshape(128, 512) for w in (
        dh(A["L2_xattn_q_w"], 16, 128), dh(kv[:, 0::2], 16, 128), kv[:, 1::2], A["L2_xattn_out_w"])], 1))
    chunks += mlp(A["L2_xattn_mlp_w1"], A["L2_xattn_mlp_w2"])
    last = [dt(w).reshape(128, -1) for w in (
        dh(A["L3_xattn_Wq"], 32, 128), A["L3_xattn_Wo"], dh(A["L3_xattn_Wk"], 8, 64), A["L3_xattn_Wv"])]
    last.append(np.zeros((128, 2048 - sum(x.shape[1] for x in last)), np.float32))
    chunks.append(np.concatenate(last, 1))
    wts = np.ascontiguousarray(np.stack(chunks))

    def pc(v):
        return v.reshape(-1, 128).T

    cs = []
    for a in (1, 2):
        for n in (f"ln{a}_scale", f"ln{a}_offset", f"bq{a}", f"bk{a}", f"bv{a}", f"bias_k{a}", f"bias_v{a}"):
            cs.append(pc(A["L0_xattn_" + n].reshape(-1)))
    cs += [pc(A["L0_xattn_ln_mlp_scale"]), pc(A["L0_xattn_ln_mlp_offset"]), pc(A["L0_xattn_b_fc1"])]
    cs += [pc(A["L1_xattn_ln2_w"]), pc(A["L1_xattn_ln2_b"]), pc(A["L1_xattn_fc_b"])]
    cs += [pc(A["L2_xattn_postnorm_w"]), np.zeros((128, 2), np.float32), pc(A["L2_xattn_mlp_b1"])]
    cs += [pc(A["L1_xattn_ln1_w"]), pc(A["L1_xattn_ln1_b"])]
    cs += [pc(dh(A["L1_xattn_q_b"], 16, 128)), pc(dh(A["L1_xattn_k_b"], 16, 128))]
    kvb = A["L2_xattn_kv_b"]
    cs += [pc(dh(A["L2_xattn_q_b"], 16, 128)), pc(dh(kvb[0::2], 16, 128))]
    kb = np.zeros((128, 2), np.float32)
    kb[0:64, 0] = dh(A["L3_xattn_bk"], 8, 64)
    cs += [pc(dh(A["L3_xattn_bq"], 32, 128)), kb]
    cols = np.ascontiguousarray(np.concatenate(cs, 1))
    vb3 = np.zeros(256, np.float32)
    vb3[:64] = A["L3_xattn_bv"]
    rows = np.stack([A["L0_xattn_bo1"], A["L0_xattn_bo2"], A["L0_xattn_b_fc2"], A["L1_xattn_v_b"],
                     A["L1_xattn_cproj_b"], A["L1_xattn_proj_b"], kvb[1::2], A["L2_xattn_out_b"],
                     A["L2_xattn_mlp_b2"], vb3, A["L3_xattn_bo"], A["L3_xattn_gamma"], A["L3_xattn_beta"]])
    rows = np.ascontiguousarray(np.broadcast_to(rows[:, None, :], (NROW, 128, 256)))
    ctx = np.ascontiguousarray(A["ctx_2048"].reshape(1024, 256).T)
    m1 = np.ascontiguousarray(np.broadcast_to(A["mask_BxS2_bf1"].view(np.uint8)[:, None, :], (4, 128, 256)))
    m2 = np.ascontiguousarray(np.broadcast_to(A["mask_BxS2_ik0"][:, None, :], (4, 128, 256)))
    m3 = np.ascontiguousarray(A["mask_Bx1xSxS2_ff0"][:, 0])
    return {"x": np.ascontiguousarray(A["x"]), "ctx": ctx,
            "mask1": m1,
            "mask2": m2, "mask3": m3,
            "wts": wts, "cols": cols, "rows": rows, "ident": np.eye(128, dtype=np.float32)}


def kernel(**inputs):
    import concourse.bacc as bacc
    import numpy as np
    from concourse.bass_utils import run_bass_kernel_spmd

    nc = bacc.Bacc("TRN2", target_bir_lowering=False, num_devices=1)
    arrays, args = {}, []
    for name, a in layouts(inputs).items():
        arrays[f"in_{name}"] = a
        args.append(nc.dram_tensor(f"in_{name}", a.shape, mybir.dt.from_np(a.dtype), kind="ExternalInput").ap())
    out = nc.dram_tensor("out_0", (4, 256, 256), F32, kind="ExternalOutput").ap()
    program(nc, *args, out)
    r = run_bass_kernel_spmd(nc, [arrays], core_ids=[0])
    return r.results[0]["out_0"]
```

```python
from contextlib import ExitStack

import concourse.bass as bass
from concourse import mybir

F32 = mybir.dt.float32
F32R = mybir.dt.float32r
BF16 = mybir.dt.bfloat16
ALU = mybir.AluOpType
ACT = mybir.ActivationFunctionType
AX = mybir.AxisListType

NB = 4
TOK = 256
CH = 2048


ORDER = {1: "STABXP", 2: "TSXAPB", 3: "STABXP"}
EVAC = {1: "DA", 2: "DA", 3: "DAD"}
XL = {1: 0, 2: 0, 3: 0}
LAGS = {1: 2, 2: 2, 3: 2}


class Ctx:

    def __init__(self, nc, stack):
        self.nc, self.stack = nc, stack
        self.sems, self.n, self.seen, self.last = {}, {}, {}, {}
        self.id = 0

    def sem(self, role):
        if role not in self.sems:
            self.sems[role] = self.stack.enter_context(self.nc.semaphore("s_" + role))
            self.n[role] = 0
        return self.sems[role]

    def sig(self, ins, role, by=1):
        s = self.sem(role)
        ins.then_inc(s, by)
        self.n[role] += by
        self.last[role if by == 16 else role.split("_")[0]] = (role, self.n[role])
        return (role, self.n[role])

    def wait(self, eng, *marks):
        for m in marks:
            if m is None:
                continue
            key = (id(eng), m[0])
            if self.seen.get(key, 0) < m[1]:
                eng.wait_ge(self.sems[m[0]], m[1])
                self.seen[key] = m[1]

    def sb(self, stack, name, shape, dt=F32):
        self.id += 1
        return stack.enter_context(self.nc.sbuf_tensor(f"{name}_{self.id}", shape, dt))


def f32(ap):
    return ap.bitcast(F32)


COLS = {}


def _cols():
    at = 0
    for a in range(2):
        for name, n in (("ln_s", 2), ("ln_o", 2), ("bq", 16), ("bk", 16), ("bv", 16),
                        ("bias_k", 16), ("bias_v", 16)):
            COLS[name, a] = (at, n)
            at += n
    for m in range(3):
        for name, n in (("m_s", 2), ("m_o", 2), ("m_b1", 8)):
            COLS[name, m] = (at, n)
            at += n
    for name, n in (("l_s", 2), ("l_o", 2)):
        COLS[name, 1] = (at, n)
        at += n
    for l in (1, 2, 3):
        for name, n in (("qb", 2), ("kb", 2)):
            COLS[name, l] = (at, n)
            at += n
    return at


NCOL = _cols()
ROWS = {n: i for i, n in enumerate(("bo0", "bo1", "b2_0", "vb1", "ob1", "b2_1", "vb2", "ob2", "b2_2",
                                    "vb3", "ob3", "gamma", "beta"))}
NROW = len(ROWS)
QSCALE = {18: 0.25, 21: 1.0 / 16.0, 24: 8.0 ** -0.5}


def program(nc, x_in, ctx_in, mask1, mask2, mask3, wts, cols_in, rows_in, ident_in, out):
    with ExitStack() as top:
        k = Ctx(nc, top)
        pe, act, dve, pool, sp = nc.tensor, nc.scalar, nc.vector, nc.gpsimd, nc.sync
        sig, wait = k.sig, k.wait

        Wt = {}

        def slots(stack, names):
            for n in names:
                Wt[n] = k.sb(stack, f"W{n}x", [128, 2 * CH], F32R)

        slots(top, (5,))
        CTh = k.sb(top, "CTh", [128, 2, NB * TOK], F32R)
        CTl = k.sb(top, "CTl", [128, 2, NB * TOK], F32R)
        X = k.sb(top, "X", [128, NB * 2, 256])
        ident = k.sb(top, "ident", [128, 128])
        cols = k.sb(top, "cols", [128, NCOL])
        small = k.sb(top, "small", [128, 64])
        neghalf = small[:, 60:62]
        stage = k.sb(top, "stage", [128, 4, 512])
        B = [top.enter_context(nc.psum_tensor(f"bank{i}", [128, 512], F32)) for i in range(8)]

        def col(name, i, j=0, n=1):
            at = COLS[name, i][0] + j
            return cols[:, at:at + n]

        ld_x = [None] * NB

        def load_x(b):
            ld_x[b] = sig(sp.dma_start(X[:, 2 * b:2 * b + 2, :], x_in[b].rearrange("(t p) d -> p t d", p=128)),
                          f"ld_x{b}", 16)

        def all_wait(*marks):
            for e in (pe, act, dve, pool, sp):
                wait(e, *marks)

        nh = sig(dve.memset(neghalf, -0.5), "nh")
        units = k.sb(top, "units", [128, 256], BF16)
        um = sig(dve.memset(units[:], 1.0), "dve_u")

        def warm(n, bank):
            wait(pe, um)
            for _ in range(n):
                pe.matmul(bank[:, 0:256], units[:, 0:128], units[:], start=True, stop=True)

        chunks = {}

        def make_loader(stage, nst, tag):
            state = {"n": 0, "free": [None] * nst}

            def load(c, j):
                r = state["n"] % nst
                state["n"] += 1
                wait(sp, *(state["free"][r] or ()))
                mark = sig(sp.dma_start(stage[:, r, :], wts[c][:, 512 * j:512 * j + 512]), f"ld_w{tag}{r}", 16)
                return r, mark

            def pieces(c, slot, scale, ncol, free):
                done = chunks[c] = [None] * ncol

                def piece(j, r, mark):
                    src = stage[:, r, :]
                    hi = Wt[slot][:, 512 * j:512 * j + 512]
                    lo = Wt[slot][:, CH + 512 * j:CH + 512 * j + 512]
                    s = scale if j == 0 else 1.0
                    wait(act, mark, *free())
                    if s != 1.0:
                        h = sig(act.activation(hi, src, ACT.Identity, scale=s), "act_whi")
                    else:
                        h = sig(act.copy(hi, src), "act_whi")
                    wait(dve, mark, h)
                    if s != 1.0:
                        l = sig(dve.scalar_tensor_tensor(out=lo, in0=src, scalar=s, in1=f32(hi),
                                                         op0=ALU.mult, op1=ALU.subtract), "dve_wlo")
                    else:
                        l = sig(dve.tensor_tensor(lo, src, f32(hi), ALU.subtract), "dve_wlo")
                    done[j] = l
                    state["free"][r] = (h, l)
                return [(lambda j=j: load(c, j), lambda r, m, j=j: piece(j, r, m)) for j in range(ncol)]
            pieces.state = state
            return pieces

        pieces = make_loader(stage, 4, "a")
        queue, loaded = [], []

        def pop(n):
            for _ in range(n):
                if loaded:
                    mark, split = loaded.pop(0)
                    split(*mark)
            while queue and len(loaded) < 4:
                load, split = queue.pop(0)
                loaded.append((load(), split))

        def boundary():
            all_wait(*k.last.values())

        def ran(work):
            while True:
                try:
                    next(work)
                except StopIteration as end:
                    return end.value

        def advance(works):
            for work in list(works):
                if next(work, "end") == "end":
                    works.remove(work)

        def ln_norm(src, eps, rms, need, scr):
            st, mv, rs, xn = scr["st"], scr["mv"], scr["rs"], scr["xn"]
            wait(dve, *need)
            wait(dve, *scr.get("xn_free", ()), *scr.get("st_free", ()))
            for t in range(2):
                m = sig(dve.bn_stats(st[:, t, :], src[:, t, :]), "dve_bn")
            wait(dve, m)
            for t in range(2):
                m = sig(dve.bn_aggr(mv[:, t, :], st[:, t, :]), "dve_bn")
            scr["st_free"] = (m,)
            if rms:
                wait(dve, m)
                m = sig(dve.tensor_tensor(rs[:, 0:2], mv[:, :, 0], mv[:, :, 0], ALU.mult), "dve_bn")
                wait(dve, m)
                m = sig(dve.tensor_tensor(mv[:, :, 1], mv[:, :, 1], rs[:, 0:2], ALU.add), "dve_bn")
            wait(pool, m, nh)
            m = sig(pool.tensor_scalar(rs[:, 2:4], mv[:, :, 1], eps, None, ALU.add), "pool_ln")
            wait(pool, m)
            m = sig(pool.tensor_tensor(rs[:, 4:6], rs[:, 2:4], neghalf, ALU.pow), "pool_ln")
            yield
            wait(dve, m)
            for t in range(2):
                if rms:
                    m = sig(dve.tensor_scalar(xn[:, t, :], src[:, t, :], rs[:, 4 + t:5 + t], None,
                                              ALU.mult), "dve_xn")
                else:
                    m = sig(dve.tensor_scalar(xn[:, t, :], src[:, t, :], mv[:, t, 0:1],
                                              rs[:, 4 + t:5 + t], ALU.subtract, ALU.mult), "dve_xn")
            return m

        def ln_turning(xn_mark, bank, bank_free, dst_h, dst_l, dst_free, s_col, o_col, scr):
            wait(pe, xn_mark, bank_free, ld_id)
            xn = hf = scr["xn"]
            for d in range(2):
                for t in range(2):
                    m = pe.transpose(bank[:, d * 256 + t * 128:d * 256 + t * 128 + 128],
                                     xn[:, t, d * 128:d * 128 + 128], ident[:])
            m = sig(m, "pe_lnT")
            yield
            wait(dve, m, ld_cols)
            for d in range(2):
                src = bank[:, d * 256:d * 256 + 256]
                if o_col is None:
                    m = sig(dve.tensor_scalar(hf[:, d, :], src, s_col(d), None, ALU.mult), "dve_hf")
                else:
                    m = sig(dve.tensor_scalar(hf[:, d, :], src, s_col(d), o_col(d), ALU.mult, ALU.add),
                            "dve_hf")
            done = m
            yield
            wait(act, m, *dst_free)
            h = sig(act.copy(dst_h, hf[:]), "act_hhi")
            wait(dve, h)
            l = sig(dve.tensor_tensor(dst_l, hf[:], f32(dst_h), ALU.subtract), "dve_hlo")
            scr["xn_free"] = (l,)
            return done, (h, l)

        def ln_scratch(st, n=""):
            return {"st": k.sb(st, "bnst", [128, 2, 6]), "mv": k.sb(st, "bnmv", [128, 2, 2]),
                    "rs": k.sb(st, "bnrs", [128, 6]), "xn": k.sb(st, "xn", [128, 2, 256])}

        def mm3(o, wh, wl, xh, xl, first, last, skip=False):
            pe.matmul(o, wh, xh, start=first, stop=False, skip_group_check=skip)
            pe.matmul(o, wh, xl, start=False, stop=False, skip_group_check=skip)
            return pe.matmul(o, wl, xh, start=False, stop=last, skip_group_check=skip)

        x_done = [None] * NB

        early = top.enter_context(ExitStack())
        slots(early, (2, 3, 4))
        earlier = early.enter_context(ExitStack())
        slots(earlier, (0, 1, 6, 7))
        with ExitStack() as st:
            QTh = k.sb(st, "QTh", [128, 2, 256], F32R)
            QTl = k.sb(st, "QTl", [128, 2, 256], F32R)
            KT = k.sb(st, "KT", [128, 2, 2, 258], F32R)
            Vh = k.sb(st, "Vh", [128, 2, 2, 256], F32R)
            Vl = k.sb(st, "Vl", [128, 2, 2, 256], F32R)
            E = k.sb(st, "E", [128, 3, 2, 258])
            PTh = k.sb(st, "PTh", [128, 2, 256], F32R)
            PTl = k.sb(st, "PTl", [128, 2, 256], F32R)
            OTh = k.sb(st, "OTh", [128, 256], F32R)
            OTl = k.sb(st, "OTl", [128, 256], F32R)
            hTh = k.sb(st, "hTh", [128, 2, 2, 256], F32R)
            hTl = k.sb(st, "hTl", [128, 2, 2, 256], F32R)
            nm = k.sb(st, "nm", [128, 4, 2])
            ls = k.sb(st, "ls", [128, 4, 2])
            rl = k.sb(st, "rl", [128, 4, 2])
            pb = k.sb(st, "pb", [128, 2, 2, 32])
            pbT = k.sb(st, "pbT", [128, 256])
            Cst = k.sb(st, "Cst", [128, 256])
            BVh = k.sb(st, "BVh", [128, 400], F32R)
            BVl = k.sb(st, "BVl", [128, 400], F32R)
            BK = k.sb(st, "BK", [128, 16, 2, 2], F32R)
            bqs = k.sb(st, "bqs", [128, 2, 16])
            bo = k.sb(st, "bo", [128, 256])
            scr = ln_scratch(st)
            SC = 1.0 / float(128.0 ** 0.5)
            accB, S0, S1, QKB, VB, PTB, OTB, MISC = B

            def inits():
                z1 = sig(pool.memset(pb[:], 0.0), "pool_ini")
                wait(pool, z1)
                m1 = sig(pool.memset(pb[:, :, :, 16:17], 1.0), "pool_ini")
                wait(pool, m1)
                return m1, sig(pool.memset(pbT[:], 0.0), "pool_ini")

            ct = [[], []]

            def ctx_pieces(half):
                cc = slice(512 * half, 512 * half + 512)

                def load(d):
                    state = pieces.state
                    r = state["n"] % 4
                    state["n"] += 1
                    wait(sp, *(state["free"][r] or ()))
                    return r, sig(sp.dma_start(stage[:, r, :], ctx_in[128 * d:128 * d + 128, cc]), f"ld_wa{r}", 16)

                def split(d, r, mark):
                    wait(act, mark)
                    h = sig(act.copy(CTh[:, d, cc], stage[:, r, :]), "act_ct")
                    wait(dve, mark, h)
                    lo = sig(dve.tensor_tensor(CTl[:, d, cc], stage[:, r, :], f32(CTh[:, d, cc]), ALU.subtract),
                             "dve_ct")
                    ct[half] += [h, lo]
                    pieces.state["free"][r] = (h, lo)
                return [(lambda d=d: load(d), lambda r, m, d=d: split(d, r, m)) for d in range(2)]

            load_x(0)
            ld_id = sig(sp.dma_start(ident[:], ident_in), "ld_id", 16)
            ld_cols = sig(sp.dma_start(cols[:], cols_in), "ld_cols", 16)
            queue += ctx_pieces(0)
            queue += pieces(0, 0, SC, 4, lambda: ())
            queue += pieces(1, 1, SC, 4, lambda: ())
            pop(0)
            pb1, pbz = inits()
            BVf = scr["xn"]

            prep = {}

            def consts(a, bv_free):
                bvf = BVf[:].rearrange("p a b -> p (a b)")[:, 0:400]
                wait(dve, *scr.get("xn_free", ()), *bv_free)
                m = sig(dve.memset(bvf, 0.0), "dve_bv")
                wait(dve, m, ld_cols)
                m = sig(dve.tensor_tensor(bvf[:, 0:18 * 15 + 1:18], col("bias_v", a, 0, 16),
                                          col("bv", a, 0, 16), ALU.subtract), "dve_bv")
                m = sig(dve.tensor_copy(bvf[:, 16:16 + 17 * 15 + 1:17], col("bv", a, 0, 16)), "dve_bv")
                wait(dve, m)
                m = sig(dve.tensor_copy(BVh[:], bvf), "dve_bv")
                wait(dve, m)
                m = sig(dve.tensor_tensor(BVl[:], bvf, f32(BVh[:]), ALU.subtract), "dve_bv")
                scr["xn_free"] = (m,)
                prep["bv", a] = m

            def key_biases(a, bk_free):
                wait(dve, *bk_free)
                if a == 0:
                    m = sig(dve.memset(f32(BK[:]), 0.0), "dve_bk")
                    wait(dve, m)
                m = sig(dve.tensor_copy(BK[:, :, 0, 0], col("bias_k", a, 0, 16)), "dve_bk")
                wait(dve, m)
                prep["bk", a] = sig(dve.tensor_tensor(BK[:, :, 1, 0], col("bias_k", a, 0, 16),
                                                      f32(BK[:, :, 0, 0]), ALU.subtract), "dve_bk")

            def load_bo(a):
                wait(sp, *prep.get("bo_free", ()))
                prep["bo", a] = sig(sp.dma_start(bo[:], rows_in[ROWS[f"bo{a}"]]), "ld_bo", 16)

            NI = 128
            T = {}

            def g(name, i):
                return T.get((name, i))

            def dec(i):
                return i // 64, (i // 16) % 4, i % 16

            def prelude(a, b):
                n = a * 4 + b
                need = (ld_x[b],) if a == 0 else (x_done[b],)
                m = yield from ln_norm(X[:, 2 * b:2 * b + 2, :], 1e-5, False, need, scr)
                yield
                free = (g("qk", 16 * (n - 2) + 15),) if n >= 2 else ()
                r, marks = yield from ln_turning(m, MISC, T.get("misc_free"), hTh[:, n % 2], hTl[:, n % 2], free,
                                   lambda d: col("ln_s", a, d), lambda d: col("ln_o", a, d), scr)
                T["misc_free"] = r
                T["hT", n] = marks
                wait(pool, m, prep["bo", a])
                m = pool.tensor_tensor(X[:, 2 * b, :], X[:, 2 * b, :], bo[:], ALU.add)
                T["xb", n] = sig(pool.tensor_tensor(X[:, 2 * b + 1, :], X[:, 2 * b + 1, :], bo[:], ALU.add),
                                 "pool_xb")
                prep["bo_free"] = (T["xb", n],)

            def stA(i):
                a, b, h = dec(i)
                c, p, o = 8 * a + h // 2, h // 2, (h % 2) * 128
                n, j = 4 * a + b, i % 2
                wait(pe, *chunks[c][0:2], *T["hT", n], *ct[b // 2], g("qk_lo", i - 1))
                for d in range(2):
                    ws = Wt[p][:, d * 256 + o:d * 256 + o + 128]
                    wl = Wt[p][:, CH + d * 256 + o:CH + d * 256 + o + 128]
                    mm3(QKB[:, 0:256], ws, wl, hTh[:, n % 2, d, :], hTl[:, n % 2, d, :], d == 0, d == 1)
                for d in range(2):
                    ws = Wt[p][:, 512 + d * 256 + o:512 + d * 256 + o + 128]
                    wl = Wt[p][:, CH + 512 + d * 256 + o:CH + 512 + d * 256 + o + 128]
                    m = mm3(QKB[:, 256:512], ws, wl, CTh[:, d, b * 256:b * 256 + 256],
                            CTl[:, d, b * 256:b * 256 + 256], d == 0, d == 1)
                T["qk", i] = sig(m, "pe_qk")

            def stA_ev(i):
                a, b, h = dec(i)
                j = i % 2
                wait(act, T["qk", i], g("s", i - 2), bqm)
                qh = sig(act.activation(QTh[:, j, :], QKB[:, 0:256], ACT.Identity, bias=bqs[:, a, h:h + 1]),
                         "act_qk")
                kh = sig(act.activation(KT[:, j, 0, 0:256], QKB[:, 256:512], ACT.Identity,
                                        bias=col("bk", a, h)), "act_qk")
                wait(dve, T["qk", i], g("s", i - 2), kh)
                dve.scalar_tensor_tensor(out=QTl[:, j, :], in0=QKB[:, 0:256], scalar=bqs[:, a, h:h + 1],
                                         in1=f32(QTh[:, j, :]), op0=ALU.add, op1=ALU.subtract)
                T["qk_lo", i] = sig(dve.scalar_tensor_tensor(
                    out=KT[:, j, 1, 0:256], in0=QKB[:, 256:512], scalar=col("bk", a, h),
                    in1=f32(KT[:, j, 0, 0:256]), op0=ALU.add, op1=ALU.subtract), "dve_qk")

            def key_column(i):
                a, b, h = dec(i)
                j = i % 2
                wait(pool, g("s", i - 2), prep["bk", a])
                T["bk", i] = sig(pool.tensor_copy(KT[:, j, :, 256:258], f32(BK[:, h])), "pool_bk")

            def stV(i):
                a, b, h = dec(i)
                p, j, t = h // 2, (i // 2) % 2, i % 2
                wait(pe, chunks[8 * a + p][2])
                if t == 0:
                    wait(pe, g("v_lo", i - 2))
                for d in range(2):
                    t0 = b * 256 + t * 128
                    m = mm3(VB[:, t * 256:t * 256 + 256], CTh[:, d, t0:t0 + 128], CTl[:, d, t0:t0 + 128],
                            Wt[p][:, 1024 + d * 256:1280 + d * 256],
                            Wt[p][:, CH + 1024 + d * 256:CH + 1280 + d * 256], d == 0, d == 1)
                if t == 1:
                    m = sig(m, "pe_v")
                    wait(act, m, g("o", i - 4))
                    vh = sig(act.copy(Vh[:, j], VB[:]), "act_v")
                    wait(dve, vh, g("o", i - 4))
                    T["v_lo", i - 1] = T["v_lo", i] = sig(
                        dve.tensor_tensor(Vl[:, j], VB[:].rearrange("p (a b) -> p a b", a=2), f32(Vh[:, j]),
                                          ALU.subtract), "dve_v")

            def stB(i):
                a, b, h = dec(i)
                j = i % 2
                wait(pe, T["qk_lo", i], T["bk", i], g("exp", i - 1))
                for t, bank in enumerate((S0, S1)):
                    qs = QTh[:, j, t * 128:t * 128 + 128]
                    ql = QTl[:, j, t * 128:t * 128 + 128]
                    m = mm3(bank[:, 0:258], qs, ql, KT[:, j, 0, :], KT[:, j, 1, :], True, True)
                T["s", i] = sig(m, "pe_s")
                r = i % 4
                wait(dve, T["s", i], g("exp", i - 4))
                for t, bank in enumerate((S0, S1)):
                    m = sig(dve.tensor_reduce(nm[:, r, t:t + 1], bank[:, 0:257], AX.X, ALU.max, negate=True),
                            "dve_max")
                    T["max", i, t] = m

            def stBx(i):
                r = i % 4
                for t, bank in enumerate((S0, S1)):
                    wait(act, T["max", i, t], g("t", i - 3), g("rl", i - 4))
                    m = sig(act.activation(E[:, i % 3, t, 0:257], bank[:, 0:257], ACT.Exp,
                                           bias=nm[:, r, t:t + 1], accum_out=ls[:, r, t:t + 1]), "act_exp")
                T["exp", i] = m

            def stB2(i):
                a, b, h = dec(i)
                r, n = i % 4, i // 16
                wait(dve, T["exp", i], g("pn", i - 4))
                T["rl", i] = sig(dve.reciprocal(rl[:, r, :], ls[:, r, :]), "dve_rl")
                wait(pool, T["rl", i], pb1, g("pbT", n - 2))
                pool.tensor_tensor(pb[:, n % 2, :, h], E[:, i % 3, :, 256], rl[:, r, :], ALU.mult)
                for t in range(2):
                    m = sig(pool.tensor_scalar(E[:, i % 3, t, 0:256], E[:, i % 3, t, 0:256],
                                               rl[:, r, t:t + 1], None, ALU.mult), "pool_pn")
                T["pn", i] = m

            def stC(i):
                wait(pe, T["pn", i], g("pt_lo", i - 1), ld_id)
                for t in range(2):
                    for s in range(2):
                        m = pe.transpose(PTB[:, s * 256 + t * 128:s * 256 + t * 128 + 128],
                                         E[:, i % 3, t, s * 128:s * 128 + 128], ident[:])
                T["t", i] = sig(m, "pe_t")
                wait(act, T["t", i], g("o", i - 1))
                m = sig(act.copy(PTh[:], PTB[:]), "act_pt")
                wait(dve, m, g("o", i - 1))
                T["pt_lo", i] = sig(dve.tensor_tensor(PTl[:], PTB[:].rearrange("p (a b) -> p a b", a=2),
                                                      f32(PTh[:]), ALU.subtract), "dve_pt")

            def stD(i):
                a, b, h = dec(i)
                j, o = (i // 2) % 2, (h % 2) * 128
                wait(pe, T["pt_lo", i], T["v_lo", i], g("ot_lo", i - 1))
                for s in range(2):
                    m = mm3(OTB[:, 0:256], Vh[:, j, s, o:o + 128], Vl[:, j, s, o:o + 128],
                            PTh[:, s, :], PTl[:, s, :], s == 0, s == 1)
                T["o", i] = sig(m, "pe_o")
                wait(act, T["o", i], g("w", i - 1))
                m = sig(act.copy(OTh[:], OTB[:, 0:256]), "act_ot")
                wait(dve, m, g("w", i - 1))
                T["ot_lo", i] = sig(dve.tensor_tensor(OTl[:], OTB[:, 0:256], f32(OTh[:]), ALU.subtract),
                                    "dve_ot")

            def stE(i):
                a, b, h = dec(i)
                n, p = i // 16, h // 2
                wait(pe, T["ot_lo", i], chunks[8 * a + p][3])
                if h == 0:
                    wait(pe, g("x", n - 1))
                o = 1536 + (h % 2) * 256
                for t in range(2):
                    m = mm3(accB[:, t * 256:t * 256 + 256], OTh[:, t * 128:t * 128 + 128],
                            OTl[:, t * 128:t * 128 + 128], Wt[p][:, o:o + 256], Wt[p][:, CH + o:CH + o + 256],
                            h == 0 and t == 0, False, skip=True)
                T["w", i] = sig(m, "pe_w")

            def turn_pb(n):
                wait(pe, T["pn", 16 * n + 15], T.get("misc_free"))
                for t in range(2):
                    m = pe.transpose(MISC[0:32, t * 128:t * 128 + 128], pb[:, n % 2, t, :], ident[:])
                T["pbT", n] = m = sig(m, "pe_pbT")
                wait(act, m, g("cc", n - 1), pbz)
                T["misc_free"] = T["pbTs", n] = sig(act.copy(pbT[0:32, :], MISC[0:32, 0:256]),
                                                            "act_pbT")

            def close(n):
                wait(pe, T["pbTs", n], T["cst", n // 4])
                for t in range(2):
                    m = pe.matmul(accB[:, t * 256:t * 256 + 256], pbT[:, t * 128:t * 128 + 128], Cst[:],
                                  start=False, stop=True, skip_group_check=True)
                T["cc", n] = sig(m, "pe_cc")
                b = n % 4
                wait(dve, T["cc", n], T["xb", n])
                T["x", n] = x_done[b] = sig(dve.tensor_tensor(
                    X[:, 2 * b:2 * b + 2, :], accB[:].rearrange("p (a b) -> p a b", a=2),
                    X[:, 2 * b:2 * b + 2, :], ALU.add), "dve_x")

            def value_biases(a):
                wait(pe, prep["bv", a], T.get("misc_free"), *chunks[8 * a + 7])
                for h in range(16):
                    o = 1536 + (h % 2) * 256
                    m = mm3(MISC[:, 0:256], BVh[:, 17 * h:17 * h + 128], BVl[:, 17 * h:17 * h + 128],
                            Wt[h // 2][:, o:o + 256], Wt[h // 2][:, CH + o:CH + o + 256], h == 0, h == 15)
                T["bvmm", a] = m = sig(m, "pe_cst")
                wait(act, m, g("cc", 4 * a - 1))
                T["misc_free"] = T["cst", a] = sig(act.copy(Cst[:], MISC[:, 0:256]), "act_cst")

            load_bo(0)
            for b in range(1, NB):
                load_x(b)
            first = prelude(0, 0)
            warm(28, QKB)
            next(first)
            pop(1)
            next(first)
            pop(1)
            wait(dve, ld_cols)
            for a in range(2):
                bqm = sig(dve.tensor_scalar(bqs[:, a, :], col("bq", a, 0, 16), SC, None, ALU.mult), "dve_ini")
            next(first)
            pop(1)
            next(first)
            pop(1)
            ran(first)
            key_biases(0, ())
            warm(25, QKB)
            stA(0)
            stA_ev(0)
            key_column(0)
            pop(3)
            preludes = []
            for t in range(NI + 4):
                if t < 12 and t % 2 == 0:
                    queue += pieces(2 + t // 2, 2 + t // 2, SC, 4, lambda: ())
                if t == 12:
                    queue += ctx_pieces(1)
                u = t - 54
                if u >= 0 and u % 2 == 0 and u // 2 < 8:
                    p = u // 2
                    queue += pieces(8 + p, p, SC, 4, lambda p=p: (T["w", 48 + 2 * p + 1],
                                                                      T["bvmm", 0]))
                if t + 1 < NI:
                    key_column(t + 1)
                u = t - 118
                if u >= 0 and u % 2 == 0 and u // 2 < 6:
                    p = u // 2
                    queue += pieces(16 + p, p, QSCALE.get(16 + p, 1.0), 4,
                                    lambda p=p: (T["w", 112 + 2 * p + 1], T["bvmm", 1]))
                if t < NI:
                    stB(t)
                    pop(1)
                if t + 1 < NI:
                    stA(t + 1)
                    stA_ev(t + 1)
                if t < NI:
                    stBx(t)
                if t < NI:
                    stV(t)
                    stB2(t)
                    pop(1)
                if t >= 4:
                    stE(t - 4)
                    if (t - 4) % 16 == 15:
                        close((t - 4) // 16)
                    if (t - 3) % 16 == 15:
                        turn_pb((t - 3) // 16)
                if 3 <= t < NI + 3:
                    stD(t - 3)
                if 2 <= t < NI + 2:
                    stC(t - 2)
                if t == 1:
                    consts(0, ())
                if t == 50:
                    consts(1, (T["bvmm", 0],))
                    load_bo(1)
                advance(preludes)
                if t % 16 == 6 and t // 16 < 7:
                    preludes.append(prelude((t // 16 + 1) // 4, (t // 16 + 1) % 4))
                if t % 64 == 15:
                    value_biases(t // 64)
                if t == 62:
                    key_biases(1, (T["bk", 63],))
            for p in range((NI + 4 - 118 + 1) // 2, 6):
                queue += pieces(16 + p, p, QSCALE.get(16 + p, 1.0), 4, lambda: (T["w", NI - 1],))
            boundary()

        def mlp(m, gelu, wa, wb, row, src, rms, src_done):
            with ExitStack() as st:
                hTh = k.sb(st, "mhTh", [128, 2, 2, 512], F32R)
                hTl = k.sb(st, "mhTl", [128, 2, 2, 512], F32R)
                G = k.sb(st, "G", [128, 2, 512])
                GH = k.sb(st, "GH", [128, 2, 512], F32R)
                GL = k.sb(st, "GL", [128, 2, 512], F32R)
                b2 = k.sb(st, "b2", [128, 256])
                scr = [ln_scratch(st), ln_scratch(st)]
                F = B[0:2]
                A2 = [B[2:4], B[4:6]]
                M = [B[6], B[7]]
                T = {}
                b2m = sig(sp.dma_start(b2[:], rows_in[row]), "ld_b2", 16)

                def norm(b):
                    g, o, sc = b // 2, (b % 2) * 256, scr[b % 2]
                    m1 = yield from ln_norm(src[:, 2 * b:2 * b + 2, :], 1e-6 if rms else 1e-5, rms,
                                            (src_done[b],), sc)
                    wait(pool, m1, b2m, x_done[b])
                    for t in range(2):
                        z = sig(pool.tensor_tensor(X[:, 2 * b + t, :], X[:, 2 * b + t, :], b2[:], ALU.add),
                                "pool_xb")
                    T["xb", b] = z
                    yield
                    T["mf", b], T["hT", b] = yield from ln_turning(
                        m1, M[b % 2], T.get(("mf", b - 2)), hTh[:, g, :, o:o + 256],
                        hTl[:, g, :, o:o + 256], (), lambda d: col("m_s", m, d),
                        None if rms else (lambda d: col("m_o", m, d)), sc)

                def fc1(i):
                    g, f = i // 8, i % 8
                    wait(pe, chunks[16 + wa][f // 4], chunks[16 + wa][2 + f // 4], *T["hT", 2 * g], *T["hT", 2 * g + 1],
                         T.get(("gelu", i - 2)))
                    for d in range(2):
                        o = d * 1024 + f * 128
                        z = mm3(F[i % 2][:], Wt[wa][:, o:o + 128], Wt[wa][:, CH + o:CH + o + 128],
                                hTh[:, g, d, :], hTl[:, g, d, :], d == 0, d == 1)
                    z = sig(z, "pe_f1")
                    wait(act, z, T.get(("gl", i - 2)))
                    T["gelu", i] = z = sig(act.activation(G[:, i % 2, :], F[i % 2][:], gelu,
                                                          bias=col("m_b1", m, f)), "act_gelu")
                    wait(dve, z, T.get(("f2", i - 2)))
                    z = sig(dve.tensor_copy(GH[:, i % 2, :], G[:, i % 2, :]), "dve_gh")
                    wait(dve, z)
                    T["gl", i] = sig(dve.tensor_tensor(GL[:, i % 2, :], G[:, i % 2, :],
                                                       f32(GH[:, i % 2, :]), ALU.subtract), "dve_gl")

                def fc2(i):
                    g, f = i // 8, i % 8
                    wait(pe, T["gl", i], chunks[16 + wb][f // 2])
                    for t in range(4):
                        z = mm3(A2[g][t // 2][:, (t % 2) * 256:(t % 2) * 256 + 256],
                                GH[:, i % 2, t * 128:t * 128 + 128], GL[:, i % 2, t * 128:t * 128 + 128],
                                Wt[wb][:, f * 256:f * 256 + 256], Wt[wb][:, CH + f * 256:CH + f * 256 + 256],
                                f == 0 and t % 2 == 0, f == 7, skip=True)
                    T["f2", i] = sig(z, "pe_f2")
                    if f == 7:
                        for b in (2 * g, 2 * g + 1):
                            wait(dve, T["f2", i], T["xb", b])
                            x_done[b] = sig(dve.tensor_tensor(
                                X[:, 2 * b:2 * b + 2, :], A2[g][b % 2][:].rearrange("p (a b) -> p a b", a=2),
                                X[:, 2 * b:2 * b + 2, :], ALU.add), "dve_x")

                first = [norm(0), norm(1)]
                pop(0)
                while first:
                    advance(first)
                pop(4)
                ahead = [norm(2)]
                for i in range(17):
                    if i == 1:
                        ahead.append(norm(3))
                    advance(ahead)
                    if i < 16:
                        fc1(i)
                    pop(2)
                    if i >= 1:
                        fc2(i - 1)
                pop(12)
                boundary()

        mlp(0, ACT.Gelu, 0, 1, ROWS["b2_0"], X, False, x_done)
        earlier.close()
        def heads(l, sl, mask_in):
            nh, d, nkv = {1: (16, 16, 16), 2: (16, 16, 16), 3: (32, 8, 8)}[l]
            nkt = 4 if l == 2 else 2
            NK = 128 * nkt
            qp, kp = (((0, 0, 0, 1, 1, 1, 2, 2, 2), (0, 1, 2, 0, 1, 2, 0, 1, 2)) if l == 3 else
                      ((0, 0, 1, 1, 0, 2), (0, 1, 0, 1, 2, 0)))
            npr = len(qp)
            R = npr * d + (0 if l == 3 else 1)
            rep_h = nh // nkv
            nm_t = 2 if l != 3 else 1
            c = 16 + {1: 2, 2: 5, 3: 8}[l]
            w = Wt[sl]
            BIG = -3.0e38
            Y = X
            with ExitStack() as st:
                if l == 2:
                    Y = k.sb(late, "Y", [128, 8, 256])
                Q = k.sb(st, "Q", [128, 2, nh, 256], BF16)
                K = k.sb(st, "K", [128, 2, nkv, NK], BF16)
                V = k.sb(st, "V", [128, 2, nkt, nkv, 32])
                qP = k.sb(st, "qP", [128, 3, 2, 256], BF16)
                kP = k.sb(st, "kP", [128, 3, 2, 256], BF16)
                qF = k.sb(st, "qF", [128, 2, 256])
                kF = k.sb(st, "kF", [128, 2, 256])
                NPT = 5 if l == 2 else 6
                hTh = k.sb(st, "hTh", [128, 2, 256], F32R)
                hTl = k.sb(st, "hTl", [128, 2, 256], F32R)
                LAG = LAGS[l]
                E = k.sb(st, "E", [128, LAG + 1, 2, NK])
                PT = k.sb(st, "PT", [128, NPT, nkt, 256])
                nm = k.sb(st, "nm", [128, 4, 2])
                OS = k.sb(st, "OS", [128, 2, nh // 4, 256])
                On = k.sb(st, "On", [128, 2, 256])
                rl = k.sb(st, "rl", [128, 2, nh])
                OTh = k.sb(st, "OTh", [128, 2, 256], F32R)
                OTl = k.sb(st, "OTl", [128, 2, 256], F32R)
                vb = k.sb(st, "vb", [128, 256])
                ob = k.sb(st, "ob", [128, 256])
                qbs = k.sb(st, "qbs", [128, 2])
                scr = ln_scratch(st) if l != 2 else None
                SB, PTB, OB, PB, MB = B[0:2], B[2:4], B[4], B[5:7], B[7]
                T = {}
                ldv = sig(sp.dma_start(vb[:], rows_in[ROWS[f"vb{l}"]]), "ld_vb", 16)
                ldo = sig(sp.dma_start(ob[:], rows_in[ROWS[f"ob{l}"]]), "ld_ob", 16)
                if l == 3:
                    gam = k.sb(st, "gam", [128, 256])
                    bet = k.sb(st, "bet", [128, 256])
                    M3 = k.sb(st, "M3", [128, 2, 2, 256])
                    Em = k.sb(st, "Em", [128, 3, 2, 256])
                    Yo = k.sb(st, "Yo", [128, 2, 2, 256])
                    ldg = sig(sp.dma_start(gam[:], rows_in[ROWS["gamma"]]), "ld_g", 16)
                    ldb = sig(sp.dma_start(bet[:], rows_in[ROWS["beta"]]), "ld_b", 16)
                else:
                    mraw = k.sb(st, "mraw", [128, 2, 256], mask_in.dtype)
                    mrep = k.sb(st, "mrep", [128, 2, 256])
                    mrow = k.sb(st, "mrow", [128, 2, NK], BF16)
                qbm = sig(dve.tensor_scalar(qbs[:], col("qb", l, 0, 2), QSCALE[c], None, ALU.mult), "dve_ini")
                ones = []
                for j in range(2):
                    for t in range(nkt):
                        vinit = sig(pool.memset(V[:, j, t], 1.0), "pool_ini")
                if l != 3:
                    if l == 2:
                        zr = sig(pool.memset(mrow[:], 0.0), "pool_ini")
                    for j in range(2):
                        wait(sp, um)
                        ones.append(sig(sp.dma_start(Q[96:97, j, :, :], units[0:nh, :]), f"ld_one{j}", 16))

                def parts(ps_mark, srcs, P_, Fr, tag, dst, sel, role, dst_free, first):
                    wait(dve, *ps_mark, T.get("F" + tag))
                    for (o, rows, ps, bias, mul) in srcs:
                        if mul is not None:
                            z = sig(dve.scalar_tensor_tensor(out=Fr[0:rows, o, :], in0=ps, scalar=bias,
                                                             in1=mul, op0=ALU.add, op1=ALU.mult), "dve_f" + tag)
                        else:
                            z = sig(dve.tensor_scalar(Fr[0:rows, o, :], ps, bias, None, ALU.add), "dve_f" + tag)
                    T["pb" + tag] = z
                    rows, no = srcs[0][1], len(srcs)
                    F_, P = Fr[0:rows, 0:no, :], [P_[0:rows, q, 0:no] for q in range(3)]
                    free = T.get("dma" + tag, ((), (), ()))
                    made = [[], [], []]

                    def spread(part, ready):
                        wait(sp, ready, dst_free)
                        for n, q in enumerate(sel):
                            if q == part:
                                made[part].append(sig(sp.dma_start(dst(n), P[part]), f"{role}{n}", 16))

                    yield
                    wait(act, z, *free[0])
                    z = sig(act.copy(P[0], F_), "act_h" + tag)
                    spread(0, z)
                    rest, name = (dve, "dve_") if first else (pool, "pool_")
                    wait(rest, z)
                    z = sig(rest.tensor_tensor(F_, F_, P[0], ALU.subtract), name + "r" + tag)
                    yield
                    wait(act, z, *free[1])
                    z = sig(act.copy(P[1], F_), "act_m" + tag)
                    spread(1, z)
                    wait(rest, z, *free[2])
                    z = T["F" + tag] = sig(rest.tensor_tensor(P[2], F_, P[1], ALU.subtract), name + "l" + tag)
                    spread(2, z)
                    T["dma" + tag] = made
                    return made[0] + made[1] + made[2]

                def prep_turn(b):
                    free = T.get(("hfree", b - 1))
                    bank = PB[1]
                    if l == 1:
                        T["xn", b] = yield from ln_norm(X[:, 2 * b:2 * b + 2, :], 1e-5, False, (x_done[b],), scr)
                        rd = T["xn", b]
                        yield
                        T["pbq"], T["hT", b] = yield from ln_turning(T["xn", b], bank, T.get("pbq"), hTh[:], hTl[:], (free,),
                                                       lambda i: col("l_s", 1, i), lambda i: col("l_o", 1, i), scr)
                    else:
                        wait(pe, x_done[b], T.get("pbq"), ld_id)
                        for e in range(2):
                            for t in range(2):
                                z = pe.transpose(bank[:, e * 256 + t * 128:e * 256 + t * 128 + 128],
                                                 X[:, 2 * b + t, e * 128:e * 128 + 128], ident[:])
                        rd = z = sig(z, "pe_xT")
                        yield
                        wait(act, z, free)
                        h = sig(act.copy(hTh[:], bank[:]), "act_hhi")
                        yield
                        wait(dve, h, free)
                        lo = sig(dve.tensor_tensor(hTl[:], bank[:].rearrange("p (a b) -> p a b", a=2), f32(hTh[:]),
                                                   ALU.subtract), "dve_hlo")
                        T["pbq"] = lo
                        T["hT", b] = (h, lo)
                    wait(pool, rd, ldo, x_done[b])
                    for t in range(2):
                        z = sig(pool.tensor_tensor(Y[:, 2 * b + t, :], X[:, 2 * b + t, :], ob[:], ALU.add), "pool_xb")
                    T["xb", b] = z
                    yield

                def prep_q(b):
                    j = b % 2
                    ps = PB[1]
                    wait(pe, *T["hT", b], *chunks[c], T.get("pbq"))
                    for m in range(2):
                        for e in range(2):
                            o = e * 256 + m * 128
                            z = mm3(ps[:, m * 256:m * 256 + 256], w[:, o:o + 128], w[:, CH + o:CH + o + 128],
                                    hTh[:, e, :], hTl[:, e, :], e == 0, e == 1)
                    z = T["hfree", b] = sig(z, "pe_q")
                    yield
                    T["Q", b] = yield from parts((z, qbm), [(m, 128, ps[:, m * 256:m * 256 + 256], qbs[:, m:m + 1], None)
                                                for m in range(2)], qP, qF, "q",
                                     lambda n: Q[n * d:n * d + d, j, :, :], qp, "dq", T.get(("S", b - 2)), b == 0)
                    yield

                def prep_mask(b):
                    j = b % 2
                    if l == 3:
                        wait(sp, T.get(("mx", (b - 1) * nh - 1, 1)))
                        T["mask", b] = sig(sp.dma_start(M3[:, j], mask_in[b].rearrange("(t p) s -> p t s", p=128)),
                                           f"ld_m{j}", 16)
                        return
                    wait(sp, T.get(("mrep", b - 2)))
                    z = sig(sp.dma_start(mraw[:, j, :], mask_in[b]), f"ld_m{j}", 16)
                    yield
                    wait(dve, z, T.get(("kmul", b - 2)), T.get(("mdma", b - 2)))
                    z = sig(dve.tensor_scalar(mrep[:, j, :], mraw[:, j, :], 0.0, None, ALU.not_equal), "dve_mk")
                    T["mrep", b] = z
                    wait(dve, z)
                    if l == 2:
                        wait(dve, zr)
                    z = sig(dve.tensor_scalar(mrow[:, j, 0:256], mrep[:, j, :], 1.0, -BIG, ALU.subtract, ALU.mult),
                            "dve_mk")
                    wait(sp, z, T.get(("S", b - 2)))
                    T["mdma", b] = sig(sp.dma_start(K[96:97, j, :, :], mrow[0:nkv, j, :]), f"dm{j}", 16)

                def prep_k(b, half):
                    j = b % 2
                    rh, rl_ = ((CTh[:, :, b * 256:b * 256 + 256], CTl[:, :, b * 256:b * 256 + 256]) if half == 0
                               else (hTh[:], hTl[:]))
                    tag = "kq"[half]
                    ps = PB[half]
                    wait(pe, *chunks[c], T.get("pb" + tag))
                    if half:
                        wait(pe, *T["hT", b])
                    for m in range(nm_t):
                        for e in range(2):
                            o = 512 + e * 256 + m * 128 if l != 3 else 1024 + e * 64
                            z = mm3(ps[:, m * 256:m * 256 + 256], w[:, o:o + 128], w[:, CH + o:CH + o + 128],
                                    rh[:, e, :], rl_[:, e, :], e == 0, e == 1)
                    z = sig(z, "pe_k" + tag)
                    if half:
                        T["hfree", b] = z
                    yield
                    rows = 128 if l != 3 else 64
                    mul = mrep[:, j, :] if l != 3 and half == 0 else None
                    srcs = [(m, rows, ps[0:rows, m * 256:m * 256 + 256], col("kb", l, m)[0:rows], mul)
                            for m in range(nm_t)]
                    P_, Fr = (kP, kF) if half == 0 else (qP, qF)
                    T["K", b, half] = yield from parts((z, T["mrep", b]) if mul is not None else (z,), srcs, P_, Fr, tag,
                                     lambda n: K[n * d:n * d + d, j, :, half * 256:half * 256 + 256],
                                     kp, f"dk{half}", T.get(("S", b - 2)), b == 0)
                    if half == 0:
                        T["kmul", b] = T["F" + tag]
                    yield

                def prep_v(b, half):
                    j = b % 2
                    lh, ll, t0 = (CTh, CTl, b * 256) if half == 0 else (hTh, hTl, 0)
                    tag = "kq"[half]
                    ps = PB[half]
                    wd = nkv * d
                    wait(pe, *chunks[c], T.get("pb" + tag))
                    for t in range(2):
                        for e in range(2):
                            o = 1024 + e * 256 if l != 3 else 1152 + e * 64
                            s = slice(t0 + t * 128, t0 + t * 128 + 128)
                            z = mm3(ps[:, t * 256:t * 256 + wd], lh[:, e, s], ll[:, e, s], w[:, o:o + wd],
                                    w[:, CH + o:CH + o + wd], e == 0, e == 1)
                    z = sig(z, "pe_v" + tag)
                    if half:
                        T["hfree", b] = z
                    yield
                    wait(dve, z, ldv, vinit, T.get(("PV", b - 2)))
                    for t in range(2):
                        z = sig(dve.tensor_tensor(
                            V[:, j, 2 * half + t, :, 0:d],
                            ps[:, t * 256:t * 256 + wd].rearrange("p (h d) -> p h d", d=d),
                            vb[:, 0:wd].rearrange("p (h d) -> p h d", d=d), ALU.add), "dve_v")
                    T["pb" + tag] = z
                    T["V", b, half] = z

                def scores(b, h):
                    i, j = b * nh + h, b % 2
                    wait(pe, *T["Q", b], *T["K", b, 0], *ones)
                    if l != 3:
                        wait(pe, T["mdma", b])
                    if l == 2:
                        wait(pe, *T["K", b, 1])
                    for t in range(2):
                        if l == 2:
                            ps, o = SB[t], 0
                            wait(pe, T.get(("ex", i - 1, t)))
                        else:
                            ps, o = SB[i % 2], t * 256
                            wait(pe, T.get(("ex", i - 2, 1)), T.get(("mx", i - 2, 1)))
                        z = pe.matmul(ps[:, o:o + NK], Q[0:R, j, h, t * 128:t * 128 + 128], K[0:R, j, h // rep_h, :],
                                      start=True, stop=True)
                        if l == 2:
                            T["s", i, t] = sig(z, "pe_s")
                    if l != 2:
                        T["s", i, 0] = T["s", i, 1] = sig(z, "pe_s")
                    T["S", b] = T["s", i, 1]
                    r = i % 4
                    if l == 1:
                        wait(dve, T["s", i, 1], T.get(("ex", i - 4, 1)))
                        z = sig(dve.tensor_reduce(nm[:, r, :], SB[i % 2][:].rearrange("p (a b) -> p a b", a=2),
                                                  AX.X, ALU.max, negate=True), "dve_mx")
                        T["mx", i, 0] = T["mx", i, 1] = z
                    for t in range(2):
                        if l == 2:
                            wait(dve, T["s", i, t], T.get(("ex", i - 4, 1)))
                            T["mx", i, t] = sig(dve.tensor_reduce(nm[:, r, t:t + 1], SB[t][:], AX.X, ALU.max,
                                                                  negate=True), "dve_mx")
                        if l == 3:
                            wait(dve, T["s", i, 1], T["mask", b], T.get(("ex", i - 3, 1)))
                            T["mx", i, t] = sig(dve.tensor_tensor_reduce(
                                out=Em[:, i % 3, t, :], in0=SB[i % 2][:, t * 256:t * 256 + 256], in1=M3[:, j, t, :],
                                scale=-1.0, scalar=3.4e38, op0=ALU.add, op1=ALU.min,
                                accum_out=nm[:, r, t:t + 1]), "dve_mx")

                def exps(b, h):
                    i = b * nh + h
                    r = i % 4
                    for t in range(2):
                        wait(act, T["mx", i, t], T.get(("T", i - LAG - 1)))
                        if l == 3:
                            src = Em[:, i % 3, t, :]
                        elif l == 2:
                            src = SB[t][:]
                        else:
                            src = SB[i % 2][:, t * 256:t * 256 + 256]
                        T["ex", i, t] = sig(act.activation(E[:, i % (LAG + 1), t, :], src, ACT.Exp, bias=nm[:, r, t:t + 1],
                                                           scale=-1.0 if l == 3 else 1.0), "act_ex")

                def turn(b, h):
                    i = b * nh + h
                    wait(pe, T["ex", i, 1])
                    for u in range(nkt // 2):
                        n = i * (nkt // 2) + u
                        bank = PTB[n % 2]
                        wait(pe, T.get(("ev", n - 2)))
                        for t in range(2):
                            for s in range(2):
                                o = (2 * u + s) * 128
                                z = pe.transpose(bank[:, s * 256 + t * 128:s * 256 + t * 128 + 128],
                                                 E[:, i % (LAG + 1), t, o:o + 128], ident[:])
                        z = sig(z, "pe_T")
                        dst = PT[:, i % NPT, 2 * u:2 * u + 2, :]
                        src = bank[:].rearrange("p (a b) -> p a b", a=2)
                        which = EVAC[l][n % len(EVAC[l])]
                        if which == "A":
                            wait(act, z, T.get(("pv", (i - NPT) // 4)))
                            T["ev", n] = sig(act.copy(dst, src), "act_ev")
                        elif which == "P":
                            wait(pool, z, T.get(("pv", (i - NPT) // 4)))
                            T["ev", n] = sig(pool.tensor_copy(dst, src), "pool_ev")
                        else:
                            wait(dve, z, T.get(("pv", (i - NPT) // 4)))
                            T["ev", n] = sig(dve.tensor_copy(dst, src), "dve_ev")
                    T["T", i] = z

                def pv(b, g):
                    i0, j = b * nh + 4 * g, b % 2
                    gi = i0 // 4
                    e0 = (i0 + 4) * (nkt // 2)
                    wait(pe, T["V", b, 0], T.get(("V", b, 1)), *[T["ev", n] for n in range(i0 * (nkt // 2), e0)], T.get(("os", gi - 1)))
                    for s in range(nkt):
                        for q in range(4):
                            z = pe.matmul(OB[32 * q:32 * q + 32, 0:256], V[:, j, s, (4 * g + q) // rep_h, :],
                                          PT[:, (i0 + q) % NPT, s, :], start=s == 0, stop=s == nkt - 1,
                                          skip_group_check=True)
                    z = T["pv", gi] = T["PV", b] = sig(z, "pe_pv")
                    wait(act, z, T.get(("post", b - 2)))
                    T["os", gi] = T["OS", b] = sig(act.copy(OS[:, j, g, :], OB[:, 0:256]), "act_os")

                def post(b):
                    j = b % 2
                    for t in range(2):
                        for u in range(nh // 16):
                            wait(pe, T["OS", b], T.get("mb"))
                            for g in range(4):
                                z = pe.transpose(MB[:, g * 128:g * 128 + 128],
                                                 OS[:, j, 4 * u + g, t * 128:t * 128 + 128], ident[:])
                            z = T["post", b] = sig(z, "pe_po")
                            yield
                            v = MB[:].rearrange("p (h c) -> p h c", c=32)
                            wait(dve, z, T.get(("on", b - 1)))
                            z = sig(dve.reciprocal(rl[:, t, 16 * u:16 * u + 16], v[:, :, d]), "dve_rl")
                            wait(dve, z)
                            z = T["mb"] = sig(dve.tensor_tensor(
                                On[:, t, 16 * d * u:16 * d * u + 16 * d].rearrange("p (h d) -> p h d", d=d),
                                v[:, :, 0:d], rl[:, t, 16 * u:16 * u + 16].unsqueeze(2).broadcast_to([128, 16, d]),
                                ALU.mult), "dve_on")
                            yield
                    wait(pe, z)
                    for e in range(2):
                        for t in range(2):
                            z = pe.transpose(MB[:, e * 256 + t * 128:e * 256 + t * 128 + 128],
                                             On[:, t, e * 128:e * 128 + 128], ident[:])
                    z = T["on", b] = sig(z, "pe_onT")
                    yield
                    wait(act, z, T.get(("c", b - 1)))
                    h_ = sig(act.copy(OTh[:], MB[:]), "act_oth")
                    yield
                    wait(dve, h_, T.get(("c", b - 1)))
                    z = sig(dve.tensor_tensor(OTl[:], MB[:].rearrange("p (a b) -> p a b", a=2), f32(OTh[:]),
                                              ALU.subtract), "dve_otl")
                    yield
                    wait(pe, z)
                    oo = 1536 if l != 3 else 512
                    for t in range(2):
                        for e in range(2):
                            o = oo + e * 256
                            z = mm3(MB[:, t * 256:t * 256 + 256], OTh[:, e, t * 128:t * 128 + 128],
                                    OTl[:, e, t * 128:t * 128 + 128], w[:, o:o + 256], w[:, CH + o:CH + o + 256],
                                    e == 0, e == 1)
                    z = T["c", b] = sig(z, "pe_c")
                    yield
                    wait(dve, z, T["xb", b])
                    T["mb"] = y_done[b] = sig(dve.tensor_tensor(
                        Y[:, 2 * b:2 * b + 2, :], MB[:].rearrange("p (a b) -> p a b", a=2),
                        Y[:, 2 * b:2 * b + 2, :], ALU.add), "dve_y")
                    if l == 3:
                        yield
                        yield from last_norm(b)

                def last_norm(b):
                    Yb, j = Y[:, 2 * b:2 * b + 2, :], b % 2
                    m = yield from ln_norm(Yb, 1e-6, False, (y_done[b],), scr)
                    xn = scr["xn"]
                    wait(pool, m, ldg, ldb, T.get(("sto", b - 2)))
                    for t in range(2):
                        z = sig(pool.tensor_tensor(Yo[:, j, t, :], xn[:, t, :], gam[:], ALU.mult), "pool_g")
                    scr["xn_free"] = (z,)
                    wait(pool, z)
                    for t in range(2):
                        z = sig(pool.tensor_tensor(Yo[:, j, t, :], Yo[:, j, t, :], bet[:], ALU.add), "pool_g")
                    wait(sp, z)
                    T["sto", b] = sig(sp.dma_start(out[b].rearrange("(t p) d -> p t d", p=128), Yo[:, j]),
                                      f"st_o{j}", 16)

                y_done = [None] * NB

                def from_ctx(b):
                    yield from prep_k(b, 0)
                    yield from prep_v(b, 0)

                def from_queries(b):
                    yield from prep_turn(b)
                    yield from prep_q(b)
                    if l == 2:
                        yield from prep_k(b, 1)
                        yield from prep_v(b, 1)

                preps = [prep_mask(0), from_queries(0), from_ctx(0)]
                while preps:
                    advance(preps)
                posts = []
                N = NB * nh
                for i in range(N + LAG + 2):
                    b, h = i // nh, i % nh
                    if h == 0 and b + 1 < NB:
                        while preps:
                            advance(preps)
                        preps = [prep_mask(b + 1), from_queries(b + 1), from_ctx(b + 1)]
                    for op in ORDER[l]:
                        if op == "T" and 0 <= i - LAG < N:
                            turn((i - LAG) // nh, (i - LAG) % nh)
                        if op == "S" and i < N:
                            scores(b, h)
                        if op == "X" and XL[l] <= i < N + XL[l]:
                            exps((i - XL[l]) // nh, (i - XL[l]) % nh)
                        v = i - LAG - 1
                        if op == "P" and 0 <= v < N and v % 4 == 3:
                            pv(v // nh, (v % nh) // 4)
                        if op == "A":
                            advance(preps)
                        if op == "B" and not (v >= 0 and v % nh == nh - 1):
                            advance(posts)
                    if v >= 0 and v % nh == nh - 1:
                        while posts:
                            advance(posts)
                        posts.append(post(v // nh))
                    if h % 2 == 0:
                        pop(1)
                while posts:
                    advance(posts)
                pop(12)
                if l == 3:
                    wait(sp, *[T["sto", b] for b in range(NB)])
                else:
                    boundary()
                return y_done, Y

        yd, _ = heads(1, 2, mask1)
        x_done = yd
        mlp(1, ACT.Gelu_apprx_tanh, 3, 4, ROWS["b2_1"], X, False, x_done)
        early.close()
        late = top.enter_context(ExitStack())
        slots(late, (6,))
        queue += pieces(22, 6, 1.0, 4, lambda: ())
        yd, Y = heads(2, 5, mask2)
        slots(late, (7,))
        queue += pieces(23, 7, 1.0, 4, lambda: ()) + pieces(24, 5, QSCALE[24], 3, lambda: ())
        mlp(2, ACT.Gelu_apprx_tanh, 6, 7, ROWS["b2_2"], Y, True, yd)
        late.close()
        heads(3, 5, mask3)


def layouts(i):
    import numpy as np
    A = {n: np.asarray(v) for n, v in i.items()}

    def dt(w):
        return w.reshape(2, 128, -1).transpose(1, 0, 2)

    chunks = []
    for a in (1, 2):
        wq, wk, wv, wo = (A[f"L0_xattn_{n}{a}"] for n in ("wq", "wk", "wv", "wo"))
        for p in range(8):
            parts = [dt(w[:, 256 * p:256 * p + 256]).reshape(128, 512) for w in (wq, wk, wv)]
            parts.append(wo[256 * p:256 * p + 256].reshape(2, 128, 256).transpose(1, 0, 2).reshape(128, 512))
            chunks.append(np.concatenate(parts, 1))

    def mlp(w1, w2):
        return [dt(w1).reshape(128, 2048), w2.reshape(8, 128, 256).transpose(1, 0, 2).reshape(128, 2048)]

    def dh(w, nh, tile):
        d = w.shape[-1] // nh
        hp = tile // d
        s = w.shape[:-1]
        w = w.reshape(*s, hp, nh // hp, d)
        return np.moveaxis(w, -3, -1).reshape(*s, nh * d)

    chunks += mlp(A["L0_xattn_w_fc1"], A["L0_xattn_w_fc2"])
    chunks.append(np.concatenate([dt(w).reshape(128, 512) for w in (
        dh(A["L1_xattn_q_w"], 16, 128), dh(A["L1_xattn_k_w"], 16, 128), A["L1_xattn_v_w"],
        A["L1_xattn_cproj_w"])], 1))
    chunks += mlp(A["L1_xattn_fc_w"], A["L1_xattn_proj_w"])
    kv = A["L2_xattn_kv_w"]
    chunks.append(np.concatenate([dt(w).reshape(128, 512) for w in (
        dh(A["L2_xattn_q_w"], 16, 128), dh(kv[:, 0::2], 16, 128), kv[:, 1::2], A["L2_xattn_out_w"])], 1))
    chunks += mlp(A["L2_xattn_mlp_w1"], A["L2_xattn_mlp_w2"])
    last = [dt(w).reshape(128, -1) for w in (
        dh(A["L3_xattn_Wq"], 32, 128), A["L3_xattn_Wo"], dh(A["L3_xattn_Wk"], 8, 64), A["L3_xattn_Wv"])]
    last.append(np.zeros((128, 2048 - sum(x.shape[1] for x in last)), np.float32))
    chunks.append(np.concatenate(last, 1))
    wts = np.ascontiguousarray(np.stack(chunks))

    def pc(v):
        return v.reshape(-1, 128).T

    cs = []
    for a in (1, 2):
        for n in (f"ln{a}_scale", f"ln{a}_offset", f"bq{a}", f"bk{a}", f"bv{a}", f"bias_k{a}", f"bias_v{a}"):
            cs.append(pc(A["L0_xattn_" + n].reshape(-1)))
    cs += [pc(A["L0_xattn_ln_mlp_scale"]), pc(A["L0_xattn_ln_mlp_offset"]), pc(A["L0_xattn_b_fc1"])]
    cs += [pc(A["L1_xattn_ln2_w"]), pc(A["L1_xattn_ln2_b"]), pc(A["L1_xattn_fc_b"])]
    cs += [pc(A["L2_xattn_postnorm_w"]), np.zeros((128, 2), np.float32), pc(A["L2_xattn_mlp_b1"])]
    cs += [pc(A["L1_xattn_ln1_w"]), pc(A["L1_xattn_ln1_b"])]
    cs += [pc(dh(A["L1_xattn_q_b"], 16, 128)), pc(dh(A["L1_xattn_k_b"], 16, 128))]
    kvb = A["L2_xattn_kv_b"]
    cs += [pc(dh(A["L2_xattn_q_b"], 16, 128)), pc(dh(kvb[0::2], 16, 128))]
    kb = np.zeros((128, 2), np.float32)
    kb[0:64, 0] = dh(A["L3_xattn_bk"], 8, 64)
    cs += [pc(dh(A["L3_xattn_bq"], 32, 128)), kb]
    cols = np.ascontiguousarray(np.concatenate(cs, 1))
    vb3 = np.zeros(256, np.float32)
    vb3[:64] = A["L3_xattn_bv"]
    rows = np.stack([A["L0_xattn_bo1"], A["L0_xattn_bo2"], A["L0_xattn_b_fc2"], A["L1_xattn_v_b"],
                     A["L1_xattn_cproj_b"], A["L1_xattn_proj_b"], kvb[1::2], A["L2_xattn_out_b"],
                     A["L2_xattn_mlp_b2"], vb3, A["L3_xattn_bo"], A["L3_xattn_gamma"], A["L3_xattn_beta"]])
    rows = np.ascontiguousarray(np.broadcast_to(rows[:, None, :], (NROW, 128, 256)))
    ctx = np.ascontiguousarray(A["ctx_2048"].reshape(1024, 256).T)
    m1 = np.ascontiguousarray(np.broadcast_to(A["mask_BxS2_bf1"].view(np.uint8)[:, None, :], (4, 128, 256)))
    m2 = np.ascontiguousarray(np.broadcast_to(A["mask_BxS2_ik0"][:, None, :], (4, 128, 256)))
    m3 = np.ascontiguousarray(A["mask_Bx1xSxS2_ff0"][:, 0])
    return {"x": np.ascontiguousarray(A["x"]), "ctx": ctx,
            "mask1": m1,
            "mask2": m2, "mask3": m3,
            "wts": wts, "cols": cols, "rows": rows, "ident": np.eye(128, dtype=np.float32)}


def kernel(**inputs):
    import concourse.bacc as bacc
    import numpy as np
    from concourse.bass_utils import run_bass_kernel_spmd

    nc = bacc.Bacc("TRN2", target_bir_lowering=False, num_devices=1)
    arrays, args = {}, []
    for name, a in layouts(inputs).items():
        arrays[f"in_{name}"] = a
        args.append(nc.dram_tensor(f"in_{name}", a.shape, mybir.dt.from_np(a.dtype), kind="ExternalInput").ap())
    out = nc.dram_tensor("out_0", (4, 256, 256), F32, kind="ExternalOutput").ap()
    program(nc, *args, out)
    r = run_bass_kernel_spmd(nc, [arrays], core_ids=[0])
    return r.results[0]["out_0"]
```
